# Optimizing a Trainium2 kernel written in Bass

```python
import numpy as np
import jax
import jax.numpy as jnp

def _softmax(x, axis=-1):
    return jax.nn.softmax(x, axis=axis)

def _gelu(x):
    return jax.nn.gelu(x, approximate=True)

def _silu(x):
    return jax.nn.silu(x)

def _sigmoid(x):
    return jax.nn.sigmoid(x)

def _layernorm(x, axis=-1, eps=1e-05):
    m = jnp.mean(x, axis=axis, keepdims=True)
    v = jnp.var(x, axis=axis, keepdims=True)
    return (x - m) / jnp.sqrt(v + eps)

def _scatter_add(tgt, idx, src, axis=0):
    return tgt.at[idx].add(src)

def _segment_sum(src, seg, n):
    return jax.ops.segment_sum(src, seg, n)
kernel_name = 'mk_perceiver_d1_seqx_r2_c3dde8'

def setup_inputs(seed: int=0):
    np.random.seed(seed)
    _w = jnp.asarray

    def _rec_inputs():
        import jax
        import jax.numpy as jnp
        _rk = jax.random.key(seed)
        x = -0.0003929 + 0.9999 * jax.random.normal(jax.random.fold_in(_rk, 1), (1, 512, 512), jnp.float32)
        _lenS = 512 - jax.random.randint(jax.random.fold_in(_rk, 7), (1,), 0, max(1, 512 // 4) + 1, jnp.int32)
        _lenS2 = 8192 - jax.random.randint(jax.random.fold_in(_rk, 8), (1,), 0, max(1, 8192 // 4) + 1, jnp.int32)
        _ctx_768P = jax.random.normal(jax.random.fold_in(_rk, 11), (1, 16, 384), jnp.float32)
        _ctx_768c = jax.random.dirichlet(jax.random.fold_in(_rk, 511), 0.3 * jnp.ones((16,), jnp.float32), (1, 8192))
        _ctx_768t = jnp.einsum('bsk,bkd->bsd', _ctx_768c, _ctx_768P)
        _ctx_768t = _ctx_768t * jax.lax.rsqrt(jnp.mean(jnp.square(_ctx_768t)) + 1e-12) * 0.953939
        ctx_768 = -0.00055796 + 0.999787 * (_ctx_768t + 0.3 * jax.random.normal(jax.random.fold_in(_rk, 611), (1, 8192, 384), jnp.float32))
        return (x, ctx_768)
    x, ctx_768 = _rec_inputs()

    def _L0_xattn_setup():
        import jax, jax.numpy as jnp
        import numpy as np
        IMAGE_DIM = 512
        TEXT_DIM = 384
        NUM_HEADS = 16
        HEAD_DIM = IMAGE_DIM // NUM_HEADS
        key = jax.random.key(seed)
        ks = jax.random.split(key, 14)
        B, N, M = (4, 2048, 256)
        s_img = 1.0 / np.sqrt(IMAGE_DIM)
        s_txt = 1.0 / np.sqrt(TEXT_DIM)
        s_ff = 1.0 / np.sqrt(2 * IMAGE_DIM)
        return {'x': jax.random.normal(ks[0], (B, N, IMAGE_DIM), jnp.float32), 'y': jax.random.normal(ks[1], (B, M, TEXT_DIM), jnp.float32), 'Wq': jax.random.normal(ks[2], (IMAGE_DIM, IMAGE_DIM), jnp.float32) * s_img, 'bq': jax.random.normal(ks[3], (IMAGE_DIM,), jnp.float32) * s_img, 'Wk': jax.random.normal(ks[4], (TEXT_DIM, IMAGE_DIM), jnp.float32) * s_txt, 'bk': jax.random.normal(ks[5], (IMAGE_DIM,), jnp.float32) * s_txt, 'Wv': jax.random.normal(ks[6], (TEXT_DIM, IMAGE_DIM), jnp.float32) * s_txt, 'bv': jax.random.normal(ks[7], (IMAGE_DIM,), jnp.float32) * s_txt, 'W1': jax.random.normal(ks[8], (IMAGE_DIM, 2 * IMAGE_DIM), jnp.float32) * s_img, 'b1': jax.random.normal(ks[9], (2 * IMAGE_DIM,), jnp.float32) * s_img, 'W2': jax.random.normal(ks[10], (2 * IMAGE_DIM, IMAGE_DIM), jnp.float32) * s_ff, 'b2': jax.random.normal(ks[11], (IMAGE_DIM,), jnp.float32) * s_ff}
    _L0_xattn_all = _L0_xattn_setup()
    _L0_xattn_in = {k: v for k, v in _L0_xattn_all.items() if k in ('Wq', 'bq', 'Wk', 'bk', 'Wv', 'bv', 'W1', 'b1', 'W2', 'b2')}
    del _L0_xattn_all

    def _L0_attn_setup():
        import jax, jax.numpy as jnp
        import numpy as np
        B, T, D, H = (4, 1024, 512, 16)
        HEAD_DIM = D // H
        LOCAL_WINDOW = 256

        def _rotate_half(t):
            t1, t2 = jnp.split(t, 2, axis=-1)
            return jnp.concatenate([-t2, t1], axis=-1)

        def _apply_rope(q, k):
            Tq, d = (q.shape[2], q.shape[3])
            half = d // 2
            theta = 1.0 / 10000.0 ** (jnp.arange(half, dtype=jnp.float32) / half)
            pos = jnp.arange(Tq, dtype=jnp.float32)
            freqs = pos[:, None] * theta[None, :]
            freqs = jnp.concatenate([freqs, freqs], axis=-1)
            cos = jnp.cos(freqs)[None, None]
            sin = jnp.sin(freqs)[None, None]
            q = q * cos + _rotate_half(q) * sin
            k = k * cos + _rotate_half(k) * sin
            return (q, k)
        key = jax.random.key(seed)
        k1, k2, k3 = jax.random.split(key, 3)
        x = jax.random.normal(k1, (B, T, D), dtype=jnp.float32)
        Wqkv = jax.random.normal(k2, (D, 3 * D), dtype=jnp.float32) * 0.02
        Wout = jax.random.normal(k3, (D, D), dtype=jnp.float32) * 0.02
        return {'x': x, 'Wqkv': Wqkv, 'Wout': Wout}
    _L0_attn_all = _L0_attn_setup()
    _L0_attn_in = {k: v for k, v in _L0_attn_all.items() if k in ('Wqkv', 'Wout')}
    del _L0_attn_all

    def _L0_ffn_setup():
        import jax, jax.numpy as jnp
        import numpy as np
        BLOCK = 16
        _GRID = jnp.array([0.0, 0.5, 1.0, 1.5, 2.0, 3.0, 4.0, 6.0], dtype=jnp.float32)
        _MID = jnp.array([0.25, 0.75, 1.25, 1.75, 2.5, 3.5, 5.0], dtype=jnp.float32)

        def fp4_quant_dequant(x):
            shape = x.shape
            xb = x.reshape(shape[:-1] + (shape[-1] // BLOCK, BLOCK))
            scale = jnp.max(jnp.abs(xb), axis=-1, keepdims=True) / 6.0
            scale = jnp.maximum(scale, jnp.float32(1e-12))
            xn = xb / scale
            idx = jnp.searchsorted(_MID, jnp.abs(xn))
            q = _GRID[idx] * jnp.sign(xn) * scale
            return q.reshape(shape)

        def fp4_linear(x, w):
            xq = fp4_quant_dequant(x)
            wq = fp4_quant_dequant(w)
            return jnp.einsum('bsk,nk->bsn', xq, wq)
        key = jax.random.key(seed)
        k1, k2, k3, k4 = jax.random.split(key, 4)
        H, I = (512, 1408)
        x = jax.random.normal(k1, (4, 2048, H), dtype=jnp.float32)
        w_gate = jax.random.normal(k2, (I, H), dtype=jnp.float32) * 0.02
        w_up = jax.random.normal(k3, (I, H), dtype=jnp.float32) * 0.02
        w_down = jax.random.normal(k4, (H, I), dtype=jnp.float32) * 0.02
        return {'x': x, 'w_gate': w_gate, 'w_up': w_up, 'w_down': w_down}
    _L0_ffn_all = _L0_ffn_setup()
    _L0_ffn_in = {k: v for k, v in _L0_ffn_all.items() if k in ('w_gate', 'w_up', 'w_down')}
    del _L0_ffn_all
    return {'x': x, 'ctx_768': ctx_768, 'L0_xattn_Wq': _L0_xattn_in['Wq'], 'L0_xattn_bq': _L0_xattn_in['bq'], 'L0_xattn_Wk': _L0_xattn_in['Wk'], 'L0_xattn_bk': _L0_xattn_in['bk'], 'L0_xattn_Wv': _L0_xattn_in['Wv'], 'L0_xattn_bv': _L0_xattn_in['bv'], 'L0_xattn_W1': _L0_xattn_in['W1'], 'L0_xattn_b1': _L0_xattn_in['b1'], 'L0_xattn_W2': _L0_xattn_in['W2'], 'L0_xattn_b2': _L0_xattn_in['b2'], 'L0_attn_Wqkv': _L0_attn_in['Wqkv'], 'L0_attn_Wout': _L0_attn_in['Wout'], 'L0_ffn_w_gate': _L0_ffn_in['w_gate'], 'L0_ffn_w_up': _L0_ffn_in['w_up'], 'L0_ffn_w_down': _L0_ffn_in['w_down']}

def reference(x, ctx_768, L0_xattn_Wq, L0_xattn_bq, L0_xattn_Wk, L0_xattn_bk, L0_xattn_Wv, L0_xattn_bv, L0_xattn_W1, L0_xattn_b1, L0_xattn_W2, L0_xattn_b2, L0_attn_Wqkv, L0_attn_Wout, L0_ffn_w_gate, L0_ffn_w_up, L0_ffn_w_down):
    import jax
    import jax.numpy as jnp

    def _L0_xattn_ref(x, y, Wq, bq, Wk, bk, Wv, bv, W1, b1, W2, b2):
        import jax, jax.numpy as jnp
        import numpy as np
        IMAGE_DIM = 512
        TEXT_DIM = 384
        NUM_HEADS = 16
        HEAD_DIM = IMAGE_DIM // NUM_HEADS
        B, N, _ = x.shape
        M = y.shape[1]
        q = (x @ Wq + bq).reshape(B, N, NUM_HEADS, HEAD_DIM)
        k = (y @ Wk + bk).reshape(B, M, NUM_HEADS, HEAD_DIM)
        v = (y @ Wv + bv).reshape(B, M, NUM_HEADS, HEAD_DIM)
        scale = 1.0 / np.sqrt(HEAD_DIM)
        scores = jnp.einsum('bnhd,bmhd->bhnm', q, k) * scale
        attn = jax.nn.softmax(scores, axis=-1)
        out = jnp.einsum('bhnm,bmhd->bnhd', attn, v).reshape(B, N, IMAGE_DIM)
        h = jax.nn.relu(out @ W1 + b1)
        return h @ W2 + b2

    def _L0_attn_ref(x, Wqkv, Wout):
        import jax, jax.numpy as jnp
        import numpy as np
        B, T, D, H = (4, 1024, 512, 16)
        HEAD_DIM = D // H
        LOCAL_WINDOW = 256

        def _rotate_half(t):
            t1, t2 = jnp.split(t, 2, axis=-1)
            return jnp.concatenate([-t2, t1], axis=-1)

        def _apply_rope(q, k):
            Tq, d = (q.shape[2], q.shape[3])
            half = d // 2
            theta = 1.0 / 10000.0 ** (jnp.arange(half, dtype=jnp.float32) / half)
            pos = jnp.arange(Tq, dtype=jnp.float32)
            freqs = pos[:, None] * theta[None, :]
            freqs = jnp.concatenate([freqs, freqs], axis=-1)
            cos = jnp.cos(freqs)[None, None]
            sin = jnp.sin(freqs)[None, None]
            q = q * cos + _rotate_half(q) * sin
            k = k * cos + _rotate_half(k) * sin
            return (q, k)
        Bx, Tx, C = x.shape
        h, d, w = (H, HEAD_DIM, LOCAL_WINDOW)
        qkv = x @ Wqkv
        q, k, v = jnp.split(qkv, 3, axis=-1)
        q = q.reshape(Bx, Tx, h, d).transpose(0, 2, 1, 3)
        k = k.reshape(Bx, Tx, h, d).transpose(0, 2, 1, 3)
        v = v.reshape(Bx, Tx, h, d).transpose(0, 2, 1, 3)
        q, k = _apply_rope(q, k)
        idx = jnp.arange(Tx)
        dist = idx[None, :] - idx[:, None]
        allowed = (dist <= 0) & (dist >= -(w - 1))
        scores = jnp.einsum('bhqd,bhkd->bhqk', q, k) / jnp.sqrt(jnp.float32(d))
        scores = jnp.where(allowed[None, None], scores, -jnp.inf)
        weights = jax.nn.softmax(scores, axis=-1)
        out = jnp.einsum('bhqk,bhkd->bhqd', weights, v)
        out = out.transpose(0, 2, 1, 3).reshape(Bx, Tx, C)
        return out @ Wout

    def _L0_ffn_ref(x, w_gate, w_up, w_down):
        import jax, jax.numpy as jnp
        import numpy as np
        BLOCK = 16
        _GRID = jnp.array([0.0, 0.5, 1.0, 1.5, 2.0, 3.0, 4.0, 6.0], dtype=jnp.float32)
        _MID = jnp.array([0.25, 0.75, 1.25, 1.75, 2.5, 3.5, 5.0], dtype=jnp.float32)

        def fp4_quant_dequant(x):
            shape = x.shape
            xb = x.reshape(shape[:-1] + (shape[-1] // BLOCK, BLOCK))
            scale = jnp.max(jnp.abs(xb), axis=-1, keepdims=True) / 6.0
            scale = jnp.maximum(scale, jnp.float32(1e-12))
            xn = xb / scale
            idx = jnp.searchsorted(_MID, jnp.abs(xn))
            q = _GRID[idx] * jnp.sign(xn) * scale
            return q.reshape(shape)

        def fp4_linear(x, w):
            xq = fp4_quant_dequant(x)
            wq = fp4_quant_dequant(w)
            return jnp.einsum('bsk,nk->bsn', xq, wq)
        gate = fp4_linear(x, w_gate)
        y = fp4_linear(x, w_up)
        h = jax.nn.silu(gate) * y
        return fp4_linear(h, w_down)
    x = x + _L0_xattn_ref(_layernorm(x, axis=-1), ctx_768, L0_xattn_Wq, L0_xattn_bq, L0_xattn_Wk, L0_xattn_bk, L0_xattn_Wv, L0_xattn_bv, L0_xattn_W1, L0_xattn_b1, L0_xattn_W2, L0_xattn_b2)
    x = x + _L0_attn_ref(_layernorm(x, axis=-1), L0_attn_Wqkv, L0_attn_Wout)
    x = x + _L0_ffn_ref(_layernorm(x, axis=-1), L0_ffn_w_gate, L0_ffn_w_up, L0_ffn_w_down)
    return x

_drawn_inputs = setup_inputs


def setup_inputs(seed=0):
    import zlib

    import numpy as np

    out = dict(_drawn_inputs(seed))
    spreads = {}
    factors = {'L0_xattn_bq': 6.703, 'L0_xattn_bk': 8.0}
    for name, (base, spread) in spreads.items():
        noise = np.random.default_rng([zlib.crc32(name.encode()), seed]).standard_normal(out[name].shape)
        drawn = base * np.exp(spread * noise) if base else spread * noise
        out[name] = jnp.asarray(drawn.astype(out[name].dtype))
    for name, factor in factors.items():
        out[name] = (out[name] * factor).astype(out[name].dtype)
    return out
```

```python
from contextlib import ExitStack

import numpy as np

import concourse.bass as bass
from concourse import mybir

ALU = mybir.AluOpType
ACT = mybir.ActivationFunctionType
AX = mybir.AxisListType
F32 = mybir.dt.float32
F16 = mybir.dt.float16
BF16 = mybir.dt.bfloat16
U32 = mybir.dt.uint32

P = 128
T = 512
D = 512
TT = T // P
DK = D // P
M = 8192
C = 384
CK = C // P
H = 16
HD = D // H
G = 4
HG = H // G
BLK = 512
NB = M // BLK
BT = BLK // P
FF = 2 * D
FM = FF // P
INNER = 1408
IK = INNER // P
WINDOW = 256
QB = 16
WSCALE = 256.0
SCALE = float(HD) ** -0.5
EPS = 1e-5

QUADS = M // BLK
PSLOTS = 4
CH = 4
CHK = M // CH
KROWS = 3 * HD

ROUND = {step: 1.5 * 2.0 ** 23 * step for step in (0.5, 1.0, 2.0)}
BELOW = 1.0 - 2.0 ** -23


class Chain:

    def __init__(self, eng, sem):
        self.eng, self.sem, self.n, self.moving = eng, sem, 0, 0

    def at(self, moving):
        self.moving = moving

    def __call__(self, ins):
        ins.then_inc(self.sem, 1)
        self.n += 1
        return ins

    def wait(self):
        self.eng.wait_ge(self.sem, self.n + self.moving)

    def link(self, ins):
        self(ins)
        self.wait()


def wait(eng, sem, value):
    if not (isinstance(value, int) and value <= 0):
        eng.wait_ge(sem, value)


def constants():
    half = HD // 2
    theta = (1.0 / np.float32(10000.0) ** (np.arange(half, dtype=np.float32) / np.float32(half))).astype(np.float32)
    freqs = np.arange(T, dtype=np.float32)[None, :] * np.tile(theta, 2 * HG)[:, None]
    rot = np.zeros((P, P), np.float32)
    for h in range(HG):
        for d in range(half):
            rot[h * HD + d + half, h * HD + d] = -1.0
            rot[h * HD + d, h * HD + d + half] = 1.0
    q, k = np.arange(P)[:, None], np.arange(P)[None, :]
    return {
        "cos": np.cos(freqs).astype(np.float32),
        "sin": np.sin(freqs).astype(np.float32),
        "rot": rot,
        "ident": np.eye(P, dtype=np.float32),
        "fold": np.tile(np.eye(HD, dtype=np.float32), (P // HD, 1)),
        "mask": np.concatenate([np.where(k <= q, 0.0, -1e30), np.where(k > q, 0.0, -1e30)], 1).astype(np.float32),
    }


def perceiver(nc, a, out):
    with ExitStack() as whole:
        def sb_in(stack, stage=""):
            return lambda name, shape, dt=F32: stack.enter_context(nc.sbuf_tensor(stage + name, shape, dt))

        def ps_in(stack, stage=""):
            return lambda name, shape, dt=F32: stack.enter_context(nc.psum_tensor(stage + name, shape, dt))

        def sem_in(stack, stage=""):
            return lambda name: stack.enter_context(nc.semaphore(stage + name))

        k_dram = nc.dram_tensor("k_scratch", [H, 2 * HD, M], F16)
        v_dram = nc.dram_tensor("v_scratch", [H, P, M // P, HD], F32)
        o_dram = nc.dram_tensor("o_scratch", [H * HD, T], F32)
        wq_dram = [nc.dram_tensor(f"fp4_{n}", [P, INNER * D // P], F32) for n in ("gate", "up", "down")]

        sb = sb_in(whole)
        x = sb("x", [P, TT, D])
        ident = sb("ident", [P, P])
        identh = sb("identh", [P, P], F16)
        ones = sb("ones", [P, HD])
        stats = sb("stats", [P, TT, 6])
        mv = sb("mv", [P, TT, 2])
        ve = sb("ve", [P, TT])
        sd = sb("sd", [P, TT])
        r0 = sb("r0", [P, TT])
        r1 = sb("r1", [P, TT])
        r2 = sb("r2", [P, TT])
        attend_stack = whole.enter_context(ExitStack())
        q_stack = sb_in(attend_stack)("q_stack", [P, H, T], F16)

        def layer_norm_vector(dve, chain, var_ready, sd_ready, k, xn, xn_ready):
            for t in range(TT):
                chain(nc.vector.bn_stats(stats[:, t, :], x[:, t, :]))
            chain.wait()
            for t in range(TT):
                chain(nc.vector.bn_aggr(mv[:, t, :], stats[:, t, :]))
            chain.wait()
            nc.vector.tensor_scalar(ve[:], mv[:, :, 1], EPS, None, ALU.add).then_inc(var_ready, 1)
            dve.wait_ge(sd_ready, k)
            dve.wait_ge(var_ready, k)
            chain.link(nc.vector.reciprocal(r0[:], sd[:]))
            chain.link(nc.vector.tensor_tensor(r1[:], r0[:], r0[:], ALU.mult))
            chain.link(nc.vector.tensor_tensor(r2[:], r1[:], ve[:], ALU.mult))
            chain.link(nc.vector.tensor_scalar(r1[:], r2[:], -0.5, 1.5, ALU.mult, ALU.add))
            chain.link(nc.vector.tensor_tensor(r2[:], r0[:], r1[:], ALU.mult))
            for t in range(TT):
                nc.vector.tensor_scalar(xn[:, t, :], x[:, t, :], mv[:, t, 0:1], r2[:, t:t + 1],
                                        ALU.subtract, ALU.mult).then_inc(xn_ready, 1)

        def layer_norm_scalar(act, var_ready, sd_ready, k):
            act.wait_ge(var_ready, k)
            nc.scalar.activation(sd[:], ve[:], ACT.Sqrt).then_inc(sd_ready, 1)

        var_ready = sem_in(whole)("var_ready")
        sd_ready = sem_in(whole)("sd_ready")
        xn_ready = sem_in(whole)("xn_ready")

        with ExitStack() as st:
            stage = "project_"
            sb, ps, sem = sb_in(st, stage), ps_in(st, stage), sem_in(st, stage)
            wq = sb("wq", [P, DK, D])
            wkv = sb("wkv", [P, 2, CK, D])
            w_hi = sb("w_hi", [P, 2, CK, D], F16)
            w_lo = sb("w_lo", [P, 2, CK, D], F16)
            bq = sb("bq", [P, G])
            bk = sb("bk", [P, G])
            bv = sb("bv", [P, D])
            b2 = sb("b2", [P, D])
            xn = sb("xn", [P, TT, D])
            xnT = sb("xnT", [P, DK, T])
            qf = sb("qf", [P, G, T])
            q_hi = sb("q_hi", [P, G, T], F16)
            q_lo = sb("q_lo", [P, G, T], F16)
            y = sb("y", [P, 2, BT, C])
            yT_hi = sb("yT_hi", [P, 2, CK, BLK], F16)
            yT_lo = sb("yT_lo", [P, 2, CK, BLK], F16)
            kf = sb("kf", [P, 2, BLK])
            k_hi = sb("k_hi", [P, 2, G, BLK], F16)
            k_lo = sb("k_lo", [P, 2, G, BLK], F16)
            v = sb("v", [P, 2, H, BT, HD])
            UN = INNER * D // P // (NB // 2)
            UB = UN // QB
            w_in = sb("w_in", [P, 3, UN])
            amax = sb("amax", [P, UB])
            qscale = sb("qscale", [P, UB])
            qinv = sb("qinv", [P, UB])
            qn = sb("qn", [P, UN])
            qa = sb("qa", [P, UN])
            q1 = sb("q1", [P, UN])
            q2 = sb("q2", [P, UN])
            q3 = sb("q3", [P, UN])
            w_out = sb("w_out", [P, 3, UN])

            yT_ps = ps("yT_ps", [P, CK, BLK])
            k_ps = ps("k_ps", [P, 2, BLK])
            v_ps = ps("v_ps", [P, 2, D])

            x_in = sem("x_in")
            cross_in = sem("cross_in")
            bias_in = sem("bias_in")
            y_in = [sem(f"y_in{u}") for u in range(2)]
            w_unit_in = [sem(f"w_unit_in{w}") for w in range(3)]
            w_unit_out = [sem(f"w_unit_out{w}") for w in range(3)]
            const_ready = sem("const_ready")
            wsplit_hi = sem("wsplit_hi")
            wsplit_lo = sem("wsplit_lo")
            turned = sem("turned")
            turned_out = sem("turned_out")
            q_ready = sem("q_ready")
            qf_ready = sem("qf_ready")
            qhi_ready = sem("qhi_ready")
            qlo_ready = sem("qlo_ready")
            q_stacked = sem("q_stacked")
            yT_ready = sem("yT_ready")
            yhi_ready = sem("yhi_ready")
            ylo_ready = sem("ylo_ready")
            k_ready = sem("k_ready")
            khi_ready = sem("khi_ready")
            kf_ready = sem("kf_ready")
            klo_ready = sem("klo_ready")
            v_ready = sem("v_ready")
            vs_ready = sem("vs_ready")
            k_out = [sem(f"k_out{u}") for u in range(2)]
            v_out = [sem(f"v_out{u}") for u in range(2)]
            k_used = sem("k_used")
            v_used = sem("v_used")
            amax_done = sem("amax_done")
            qinv_ready = sem("qinv_ready")
            qn_ready = sem("qn_ready")
            q_done = sem("q_done")
            wq_ready = sem("wq_ready")
            dve_chain = sem("dve_chain_p")

            y_view = a["ctx_768"][0].rearrange("(b p t) c -> b p t c", p=P, t=BT)
            k_hi_view = k_dram[:, 0:HD, :].rearrange("(g i) d k -> i d g k", i=HG)
            k_lo_view = k_dram[:, HD:2 * HD, :].rearrange("(g i) d k -> i d g k", i=HG)
            v_view = v_dram[:].rearrange("h p t d -> p h (t d)")
            w_flat = [a[n].rearrange("(p r) c -> p (r c)", p=P) if n != "L0_ffn_w_down"
                      else a[n].rearrange("(p r) c -> p (r c)", p=P)
                      for n in ("L0_ffn_w_gate", "L0_ffn_w_up", "L0_ffn_w_down")]

            def weights_pairs(w):
                return w_hi[:, w], w_lo[:, w]

            block = st.enter_context(nc.Block())

            @block.sync
            def _(sp):
                sp.dma_start(x[:], a["x"][0].rearrange("(t p) d -> p t d", p=P)).then_inc(x_in, 16)
                sp.dma_start(ident[:], a["c_ident"]).then_inc(x_in, 16)
                sp.dma_start(y[:, 0], y_view[0]).then_inc(y_in[0], 16)
                sp.dma_start(wkv[:, 0], a["L0_xattn_Wk"].rearrange("(k p) n -> p k n", p=P)).then_inc(cross_in, 16)
                sp.dma_start(wkv[:, 1], a["L0_xattn_Wv"].rearrange("(k p) n -> p k n", p=P)).then_inc(cross_in, 16)
                sp.dma_start(wq[:], a["L0_xattn_Wq"].rearrange("(k p) n -> p k n", p=P)).then_inc(cross_in, 16)
                with nc.allow_non_contiguous_dma(reason="biases, one to a partition"):
                    sp.dma_start(bq[:], a["L0_xattn_bq"].rearrange("(g p) -> p g", p=P)).then_inc(bias_in, 16)
                    sp.dma_start(bk[:], a["L0_xattn_bk"].rearrange("(g p) -> p g", p=P)).then_inc(bias_in, 16)
                sp.dma_start(bv[:], a["L0_xattn_bv"].partition_broadcast(P)).then_inc(bias_in, 16)
                sp.dma_start(b2[:], a["L0_xattn_b2"].partition_broadcast(P)).then_inc(bias_in, 16)
                sp.dma_start(y[:, 1], y_view[1]).then_inc(y_in[1], 16)
                sp.wait_ge(qhi_ready, G)
                sp.wait_ge(qlo_ready, G)
                for i in range(HG):
                    heads = q_stack[:].rearrange("p (g i) t -> p i g t", i=HG)
                    rows = slice(i * HD, (i + 1) * HD)
                    sp.dma_start(heads[0:HD, i], q_hi[rows]).then_inc(q_stacked, 16)
                    sp.dma_start(heads[HD:2 * HD, i], q_hi[rows]).then_inc(q_stacked, 16)
                    sp.dma_start(heads[2 * HD:3 * HD, i], q_lo[rows]).then_inc(q_stacked, 16)

                def block_dmas(i, u, last):
                    if not last:
                        sp.wait_ge(yT_ready, 2 * i + u + 1)
                        sp.dma_start(y[:, u], y_view[2 * i + u + 2]).then_inc(y_in[u], 16)
                    sp.wait_ge(klo_ready, (2 * i + u + 1) * G)
                    sp.wait_ge(khi_ready, (2 * i + u + 1) * G)
                    for s in range(HG):
                        rows = slice(s * HD, (s + 1) * HD)
                        keys = bass.ds((2 * i + u) * BLK, BLK)
                        sp.dma_start(k_hi_view[s, :, :, keys], k_hi[rows, u]).then_inc(k_out[u], 16)
                        sp.dma_start(k_lo_view[s, :, :, keys], k_lo[rows, u]).then_inc(k_out[u], 16)
                    sp.wait_ge(vs_ready, (2 * i + u + 1) * BT)
                    sp.dma_start(v_view[:, :, bass.ds((2 * i + u) * BT * HD, BT * HD)],
                                 v[:, u].rearrange("p h t d -> p h (t d)")).then_inc(v_out[u], 16)

                def unit_load(i, w):
                    sp.wait_ge(amax_done, 3 * i + w - 2)
                    sp.wait_ge(qn_ready, 3 * i + w - 2)
                    sp.dma_start(w_in[:, w], w_flat[w][:, bass.ds(i * UN, UN)]).then_inc(w_unit_in[w], 16)

                def unit_store(i, w):
                    sp.wait_ge(wq_ready, 3 * i + w + 1)
                    sp.dma_start(wq_dram[w][:, bass.ds(i * UN, UN)], w_out[:, w]).then_inc(w_unit_out[w], 16)

                for w in range(3):
                    sp.dma_start(w_in[:, w], w_flat[w][:, 0:UN]).then_inc(w_unit_in[w], 16)
                with sp.Fori(0, NB // 2 - 1) as i:
                    block_dmas(i, 0, False)
                    block_dmas(i, 1, False)
                    for w in range(3):
                        unit_store(i, w)
                        unit_load(i + 1, w)
                block_dmas(NB // 2 - 1, 0, True)
                block_dmas(NB // 2 - 1, 1, True)
                for w in range(3):
                    unit_store(NB // 2 - 1, w)
                sp.wait_ge(q_stacked, 16 * 3 * HG)
                for u in range(2):
                    sp.wait_ge(k_out[u], NB // 2 * 2 * HG * 16)
                    sp.wait_ge(v_out[u], NB // 2 * 16)
                for w in range(3):
                    sp.wait_ge(w_unit_out[w], NB // 2 * 16)

            @block.gpsimd
            def _(pool):
                nc.gpsimd.memset(ones[:], 1.0).then_inc(const_ready, 1)

                def unit(i, w):
                    pool.wait_ge(w_unit_in[w], 16 * (i + 1))
                    pool.wait_ge(qinv_ready, 3 * i + w + 1)
                    pool.wait_ge(q_done, 3 * i + w)
                    blocks = w_in[:, w].rearrange("p (b e) -> p b e", e=QB)
                    nc.gpsimd.tensor_tensor(qn[:].rearrange("p (b e) -> p b e", e=QB), blocks,
                                            qinv[:].unsqueeze(2).to_broadcast([P, UB, QB]),
                                            ALU.mult).then_inc(qn_ready, 1)
                    pool.wait_ge(q_done, 3 * i + w + 1)
                    pool.wait_ge(w_unit_out[w], 16 * i)
                    nc.gpsimd.tensor_tensor(w_out[:, w].rearrange("p (b e) -> p b e", e=QB),
                                            q3[:].rearrange("p (b e) -> p b e", e=QB),
                                            qscale[:].unsqueeze(2).to_broadcast([P, UB, QB]),
                                            ALU.mult).then_inc(wq_ready, 1)

                with pool.Fori(0, NB // 2) as i:
                    for w in range(3):
                        unit(i, w)

            @block.scalar
            def _(act):
                act.wait_ge(cross_in, 48)
                for w in range(2):
                    nc.scalar.activation(w_hi[:, w], wkv[:, w], ACT.Copy, scale=WSCALE).then_inc(wsplit_hi, 1)
                layer_norm_scalar(act, var_ready, sd_ready, 1)
                act.wait_ge(yT_ready, 1)
                nc.scalar.activation(yT_hi[:, 0], yT_ps[:], ACT.Copy).then_inc(yhi_ready, 1)
                act.wait_ge(bias_in, 64)
                for g in range(G):
                    act.wait_ge(q_ready, g + 1)
                    nc.scalar.activation(qf[:, g], k_ps[:, g % 2], ACT.Identity, bias=bq[:, g:g + 1]).then_inc(qf_ready, 1)
                    nc.scalar.activation(q_hi[:, g], k_ps[:, g % 2], ACT.Identity, bias=bq[:, g:g + 1]).then_inc(qhi_ready, 1)

                def keys_out(i, u):
                    for g in range(G):
                        n = (2 * i + u) * G + g
                        act.wait_ge(k_ready, n + 1)
                        if g == 0:
                            act.wait_ge(k_out[u], i * 2 * HG * 16)
                        act.wait_ge(klo_ready, n - 1 if g >= 2 else (2 * i + u) * G)
                        nc.scalar.activation(kf[:, g % 2], k_ps[:, g % 2], ACT.Identity, bias=bk[:, g:g + 1],
                                             scale=1.0 / WSCALE).then_inc(kf_ready, 1)
                        nc.scalar.activation(k_hi[:, u, g], k_ps[:, g % 2], ACT.Identity, bias=bk[:, g:g + 1],
                                             scale=1.0 / WSCALE).then_inc(khi_ready, 1)

                def y_high(i, u):
                    act.wait_ge(yT_ready, 2 * i + u + 2)
                    act.wait_ge(v_ready, (2 * i + u) * BT)
                    nc.scalar.activation(yT_hi[:, 1 - u], yT_ps[:], ACT.Copy).then_inc(yhi_ready, 1)

                with act.Fori(0, NB // 2 - 1) as i:
                    for u in range(2):
                        keys_out(i, u)
                        y_high(i, u)
                keys_out(NB // 2 - 1, 0)
                y_high(NB // 2 - 1, 0)
                keys_out(NB // 2 - 1, 1)

            @block.vector
            def _(dve):
                chain = Chain(dve, dve_chain)
                dve.wait_ge(x_in, 32)
                nc.vector.tensor_copy(identh[:], ident[:]).then_inc(const_ready, 1)
                layer_norm_vector(dve, chain, var_ready, sd_ready, 1, xn, xn_ready)
                dve.wait_ge(cross_in, 48)
                dve.wait_ge(wsplit_hi, 2)
                for w in range(2):
                    nc.vector.scalar_tensor_tensor(out=w_lo[:, w].rearrange("p k n -> p (k n)"),
                                                   in0=wkv[:, w].rearrange("p k n -> p (k n)"), scalar=WSCALE,
                                                   in1=w_hi[:, w].rearrange("p k n -> p (k n)"),
                                                   op0=ALU.mult, op1=ALU.subtract).then_inc(wsplit_lo, 1)
                dve.wait_ge(yhi_ready, 1)
                nc.vector.tensor_tensor(yT_lo[:, 0], yT_ps[:], yT_hi[:, 0], ALU.subtract).then_inc(ylo_ready, 1)
                for k in range(DK):
                    dve.wait_ge(turned, k + 1)
                    nc.vector.tensor_copy(xnT[:, k], v_ps[:, k % 2]).then_inc(turned_out, 1)
                for g in range(G):
                    dve.wait_ge(qf_ready, g + 1)
                    dve.wait_ge(qhi_ready, g + 1)
                    nc.vector.tensor_tensor(q_lo[:, g], qf[:, g], q_hi[:, g], ALU.subtract).then_inc(qlo_ready, 1)
                dve.wait_ge(bias_in, 64)
                dve.wait_ge(xn_ready, TT)
                chain.link(nc.vector.tensor_tensor(x[:], x[:], b2[:].unsqueeze(1).to_broadcast([P, TT, D]), ALU.add))
                start = chain.n

                def key_low(i, u, g):
                    n = (2 * i + u) * G + g
                    dve.wait_ge(kf_ready, n + 1)
                    dve.wait_ge(khi_ready, n + 1)
                    nc.vector.tensor_tensor(k_lo[:, u, g], kf[:, g % 2], k_hi[:, u, g], ALU.subtract).then_inc(klo_ready, 1)

                def value_out(i, u, t):
                    dve.wait_ge(v_ready, (2 * i + u) * BT + t + 1)
                    if t == 0:
                        dve.wait_ge(v_out[u], i * 16)
                    nc.vector.scalar_tensor_tensor(out=v[:, u, :, t, :],
                                                   in0=v_ps[:, t % 2].rearrange("p (h d) -> p h d", d=HD),
                                                   scalar=1.0 / WSCALE, in1=bv[:].rearrange("p (h d) -> p h d", d=HD),
                                                   op0=ALU.mult, op1=ALU.add).then_inc(vs_ready, 1)

                def y_low(i, u):
                    dve.wait_ge(yhi_ready, 2 * i + u + 2)
                    nc.vector.tensor_tensor(yT_lo[:, 1 - u], yT_ps[:], yT_hi[:, 1 - u], ALU.subtract).then_inc(ylo_ready, 1)

                def scales(i, w):
                    dve.wait_ge(w_unit_in[w], 16 * (i + 1))
                    nc.vector.tensor_reduce(amax[:], w_in[:, w].rearrange("p (b e) -> p b e", e=QB), AX.X, ALU.max,
                                            apply_absolute_value=True).then_inc(amax_done, 1)
                    dve.wait_ge(amax_done, 3 * i + w + 1)
                    dve.wait_ge(wq_ready, 3 * i + w)
                    chain.link(nc.vector.tensor_scalar(qscale[:], amax[:], 1.0 / 6.0, 1e-12, ALU.mult, ALU.max))
                    chain.link(nc.vector.reciprocal(qinv[:], qscale[:]))
                    nc.vector.tensor_scalar(qinv[:], qinv[:], BELOW, None, ALU.mult).then_inc(qinv_ready, 1)

                def grid_parts(i, w):
                    dve.wait_ge(qn_ready, 3 * i + w + 1)
                    chain.link(nc.vector.tensor_scalar(qa[:].bitcast(U32), qn[:].bitcast(U32), 0x7FFFFFFF, None,
                                                       ALU.bitwise_and))
                    chain(nc.vector.tensor_scalar(q1[:], qa[:], 2.0, ROUND[0.5], ALU.min, ALU.add))
                    chain.link(nc.vector.tensor_scalar(q2[:], qa[:], 2.0, 4.0, ALU.max, ALU.min))
                    chain.link(nc.vector.tensor_scalar(q2[:], q2[:], ROUND[1.0], -ROUND[1.0], ALU.add, ALU.add))

                def grid_sum(i, w):
                    chain.link(nc.vector.tensor_scalar(qa[:], qa[:], 4.0, ROUND[2.0], ALU.max, ALU.add))
                    chain.link(nc.vector.scalar_tensor_tensor(out=q1[:], in0=q1[:], scalar=ROUND[0.5], in1=q2[:],
                                                              op0=ALU.subtract, op1=ALU.add))
                    dve.wait_ge(wq_ready, 3 * i + w)
                    chain.link(nc.vector.scalar_tensor_tensor(out=q1[:], in0=qa[:], scalar=ROUND[2.0] + 6.0, in1=q1[:],
                                                              op0=ALU.subtract, op1=ALU.add))
                    nc.vector.scalar_tensor_tensor(out=q3[:].bitcast(U32), in0=qn[:].bitcast(U32), scalar=0x80000000,
                                                   in1=q1[:].bitcast(U32), op0=ALU.bitwise_and,
                                                   op1=ALU.bitwise_or).then_inc(q_done, 1)

                PER = 3 * 9

                def two_blocks(i, last):
                    chain.at(i * PER)
                    chain.n = start
                    filler = []
                    for w in range(3):
                        filler += [(scales, w), (grid_parts, w), (grid_sum, w)]
                    filler = iter(filler + [None] * 3)

                    def fill():
                        f = next(filler)
                        if f:
                            f[0](i, f[1])

                    for u in range(2):
                        for g in range(G):
                            key_low(i, u, g)
                            if g % 2 == 1:
                                fill()
                        if not (last and u == 1):
                            y_low(i, u)
                        for t in range(BT):
                            value_out(i, u, t)
                            fill()
                    assert chain.n - start == PER, chain.n - start

                with dve.Fori(0, NB // 2 - 1) as i:
                    two_blocks(i, False)
                two_blocks(NB // 2 - 1, True)

            @block.tensor
            def _(pe):
                def turn_y(b, u):
                    pe.wait_ge(y_in[u], b)
                    for t in range(BT):
                        for c in range(CK):
                            last = nc.tensor.transpose(yT_ps[:, c, t * P:(t + 1) * P], y[:, u, t, c * P:(c + 1) * P],
                                                       ident[:])
                    last.then_inc(yT_ready, 1)

                pe.wait_ge(x_in, 32)
                turn_y(16, 0)
                pe.wait_ge(xn_ready, TT)
                for k in range(DK):
                    if k >= 2:
                        pe.wait_ge(turned_out, k - 1)
                    for t in range(TT):
                        last = nc.tensor.transpose(v_ps[:, k % 2, t * P:(t + 1) * P], xn[:, t, k * P:(k + 1) * P], ident[:])
                    last.then_inc(turned, 1)
                pe.wait_ge(turned_out, DK)
                pe.wait_ge(cross_in, 48)
                for g in range(G):
                    if g >= 2:
                        pe.wait_ge(qhi_ready, g - 1)
                    for k in range(DK):
                        last = nc.tensor.matmul(k_ps[:, g % 2], wq[:, k, g * P:(g + 1) * P], xnT[:, k],
                                                start=k == 0, stop=k == DK - 1)
                    last.then_inc(q_ready, 1)
                pe.wait_ge(qhi_ready, G)
                pe.wait_ge(wsplit_hi, 2)
                pe.wait_ge(wsplit_lo, 2)

                def keys(i, u):
                    pe.wait_ge(yhi_ready, 2 * i + u + 1)
                    pe.wait_ge(ylo_ready, 2 * i + u + 1)
                    for g in range(G):
                        n = (2 * i + u) * G + g
                        pe.wait_ge(khi_ready, n - 1 if g >= 2 else (2 * i + u) * G)
                        cols = slice(g * P, (g + 1) * P)
                        for k in range(CK):
                            nc.tensor.matmul(k_ps[:, g % 2], w_hi[:, 0, k, cols], yT_hi[:, u, k], start=k == 0, stop=False)
                            nc.tensor.matmul(k_ps[:, g % 2], w_hi[:, 0, k, cols], yT_lo[:, u, k], start=False, stop=False)
                            last = nc.tensor.matmul(k_ps[:, g % 2], w_lo[:, 0, k, cols], yT_hi[:, u, k], start=False,
                                                    stop=k == CK - 1)
                        last.then_inc(k_ready, 1)

                def values(i, u):
                    for t in range(BT):
                        n = (2 * i + u) * BT + t
                        pe.wait_ge(vs_ready, n - 1 if t >= 2 else (2 * i + u) * BT)
                        cols = slice(t * P, (t + 1) * P)
                        for k in range(CK):
                            nc.tensor.matmul(v_ps[:, t % 2], yT_hi[:, u, k, cols], w_hi[:, 1, k], start=k == 0, stop=False)
                            nc.tensor.matmul(v_ps[:, t % 2], yT_hi[:, u, k, cols], w_lo[:, 1, k], start=False, stop=False)
                            last = nc.tensor.matmul(v_ps[:, t % 2], yT_lo[:, u, k, cols], w_hi[:, 1, k], start=False,
                                                    stop=k == CK - 1)
                        last.then_inc(v_ready, 1)

                def next_y(i, u):
                    pe.wait_ge(ylo_ready, 2 * i + u + 1)
                    turn_y(16 * (i + 1 + u), 1 - u)

                with pe.Fori(0, NB // 2 - 1) as i:
                    for u in range(2):
                        keys(i, u)
                        next_y(i, u)
                        values(i, u)
                i = NB // 2 - 1
                keys(i, 0)
                next_y(i, 0)
                values(i, 0)
                keys(i, 1)
                values(i, 1)

        with ExitStack() as st:
            stage = "attend_"
            sb, ps, sem = sb_in(st, stage), ps_in(st, stage), sem_in(st, stage)
            k_stack = sb("k_stack", [P, 2, M], F16)
            vh = sb("vh", [P, 2, M // P, HD])
            prob = sb("prob", [P, PSLOTS, BT, T])
            sum_dve = sb("sum_dve", [P, 2, 2, T])
            sum_pool = sb("sum_pool", [P, 2, 2, T])
            part_max = sb("part_max", [P, 2, TT, M // 1024])
            neg_max = sb("neg_max", [P, 2, TT], F16)
            pv_sum = sb("pv_sum", [P, 2, T])
            recip = sb("recip", [P, P])
            o_out = sb("o_out", [P, 2, P])
            fold = sb("fold", [P, HD])

            s_ps = ps("s_ps", [P, 2, T])
            pre_ps = ps("pre_ps", [P, 2, 2, BLK])
            pv_ps = ps("pv_ps", [P, T])
            misc_ps = ps("misc_ps", [P, T])

            fold_in = sem("fold_in")
            ones_row = sem("ones_row")
            k_in = [[sem(f"k_in{s}{c}") for c in range(CH)] for s in range(2)]
            v_in = [sem(f"v_in{s}") for s in range(2)]
            pre_ready = sem("pre_ready")
            pre_read = sem("pre_read")
            max_ready = sem("max_ready")
            row_ready = sem("row_ready")
            row_set = sem("row_set")
            s_ready = sem("s_ready")
            p_ready = sem("p_ready")
            pv_done = sem("pv_done")
            dve_summed = sem("dve_summed")
            pool_summed = sem("pool_summed")
            pv_read = sem("pv_read")
            den_ready = sem("den_ready")
            recip_ready = sem("recip_ready")
            o_ready = sem("o_ready")
            o_scaled = sem("o_scaled")
            o_stored = [sem(f"o_stored{s}") for s in range(2)]

            o_view = o_dram[:].rearrange("(h d) (t c) -> h t d c", d=HD, c=P)

            def quad_no(i, s, q):
                return 2 * QUADS * i + QUADS * s + q

            block = st.enter_context(nc.Block())
            LASTPAIR = H // 2 - 1

            @block.sync
            def _(sp):
                sp.dma_start(fold[:], a["c_fold"]).then_inc(fold_in, 16)

                def load_keys(h, s, c):
                    keys = slice(c * CHK, (c + 1) * CHK)
                    sp.dma_start(k_stack[0:2 * HD, s, keys], k_dram[h, :, keys]).then_inc(k_in[s][c], 16)
                    sp.dma_start(k_stack[2 * HD:3 * HD, s, keys], k_dram[h, 0:HD, keys]).then_inc(k_in[s][c], 16)

                def load_values(h, s):
                    sp.dma_start(vh[:, s], v_dram[h]).then_inc(v_in[s], 16)

                for s in range(2):
                    for c in range(CH):
                        load_keys(s, s, c)
                    load_values(s, s)

                def head(i, s, loads):
                    h = 2 * i + s
                    for c in range(CH):
                        if loads:
                            sp.wait_ge(p_ready, BT * (quad_no(i, s, QUADS // CH * (c + 1) - 1) + 1))
                            load_keys(h + 2, s, c)
                        if c == 1:
                            store_o(i, s)
                    if loads:
                        sp.wait_ge(pv_done, QUADS * (h + 1))
                        load_values(h + 2, s)

                def store_o(i, s):
                    if s == 0 and isinstance(i, int) and i == 0:
                        return
                    h = 2 * i + s - 1
                    sp.wait_ge(o_scaled, h + 1)
                    for t in range(TT):
                        sp.dma_start(o_view[h, t], o_out[t * HD:(t + 1) * HD, 1 - s]).then_inc(o_stored[1 - s], 16)

                head(0, 0, True)
                head(0, 1, True)
                with sp.Fori(1, LASTPAIR) as i:
                    head(i, 0, True)
                    head(i, 1, True)
                head(LASTPAIR, 0, False)
                head(LASTPAIR, 1, False)
                store_o(LASTPAIR + 1, 0)
                for s in range(2):
                    sp.wait_ge(o_stored[s], 16 * TT * H // 2)

            @block.tensor
            def _(pe):
                def pre(i, s, part, seen):
                    h = 2 * i + s
                    c = part // 2
                    if part % 4 == 0:
                        pe.wait_ge(k_in[s][part // 4], 32 * (i + 1))
                    def slot(b):
                        tt = 2 * (part % 2) + b
                        wait(pe, pre_read, seen * 2 + b - 1)
                        for w in range(2):
                            keys = slice(1024 * c + BLK * w, 1024 * c + BLK * (w + 1))
                            last = nc.tensor.matmul(pre_ps[:, b, w], q_stack[0:KROWS, h, tt * P:(tt + 1) * P],
                                                    k_stack[0:KROWS, s, keys], start=True, stop=True)
                        last.then_inc(pre_ready, 1)
                    return slot

                def row(i, s):
                    pe.wait_ge(max_ready, 2 * i + s + 1)
                    for t in range(TT):
                        last = nc.tensor.matmul(misc_ps[KROWS:KROWS + 1, t * P:(t + 1) * P],
                                                neg_max[:, s, t:t + 1], identh[:], start=True, stop=True)
                    last.then_inc(row_ready, 1)

                def scores(i, s, q, t):
                    h = 2 * i + s
                    if q == 0 and t == 0:
                        pe.wait_ge(row_set, h + 1)
                    n = BT * quad_no(i, s, q) + t
                    wait(pe, p_ready, n - 1)
                    key = (BT * q + t) * P
                    last = nc.tensor.matmul(s_ps[:, t % 2], k_stack[0:KROWS + 1, s, key:key + P],
                                            q_stack[0:KROWS + 1, h, :], start=True, stop=True)
                    last.then_inc(s_ready, 1)

                def weighted(i, s, q):
                    h = 2 * i + s
                    if q == 0:
                        pe.wait_ge(v_in[s], 16 * (i + 1))
                        wait(pe, pv_read, h)
                    pe.wait_ge(p_ready, BT * (quad_no(i, s, q) + 1))
                    for t in range(BT):
                        last = nc.tensor.matmul(pv_ps[t * HD:(t + 1) * HD, :], vh[:, s, BT * q + t, :],
                                                prob[:, q % PSLOTS, t, :], start=q == 0, stop=q == QUADS - 1)
                    last.then_inc(pv_done, 1)

                def denominator(i, s):
                    h = 2 * i + s
                    pe.wait_ge(dve_summed, QUADS * (h + 1))
                    pe.wait_ge(pool_summed, QUADS * (h + 1))
                    parts = [sum_dve[:, s, 0], sum_dve[:, s, 1], sum_pool[:, s, 0], sum_pool[:, s, 1]]
                    for n, part in enumerate(parts):
                        for t in range(TT):
                            last = nc.tensor.matmul(misc_ps[t * HD:(t + 1) * HD, 0:P], ones[:], part[:, t * P:(t + 1) * P],
                                                    start=n == 0, stop=n == len(parts) - 1)
                    last.then_inc(den_ready, 1)

                def output(i, s):
                    h = 2 * i + s
                    pe.wait_ge(recip_ready, h + 1)
                    pe.wait_ge(pv_read, h + 1)
                    for t in range(TT):
                        last = nc.tensor.matmul(misc_ps[t * HD:(t + 1) * HD, 0:P], fold[:], pv_sum[:, s, t * P:(t + 1) * P],
                                                start=True, stop=True)
                    last.then_inc(o_ready, 1)

                def head(i, s, first, last):
                    h = 2 * i + s
                    before = (i, 0) if s else (i - 1, 1)
                    after = (i, 1) if s == 0 else (i + 1, 0)
                    for q in range(QUADS):
                        if q < QUADS - 2:
                            slot = pre(*after, q + 2, QUADS * (h + 1) + q + 2) if last >= 1 else None
                        else:
                            slot = pre(i + 1, s, q - (QUADS - 2), QUADS * (h + 1) + q + 2) if last >= 2 else None
                        if slot:
                            slot(0)
                        scores(i, s, q, 0)
                        scores(i, s, q, 1)
                        if slot:
                            slot(1)
                        scores(i, s, q, 2)
                        scores(i, s, q, 3)
                        if q >= 1:
                            weighted(i, s, q - 1)
                        elif not first:
                            weighted(*before, QUADS - 1)
                        if q == 2 and not first:
                            denominator(*before)
                        if q == 5 and not first:
                            output(*before)
                        if q == QUADS - 2 and last >= 1:
                            wait(pe, o_scaled, h)
                            row(*after)

                pe.wait_ge(fold_in, 16)
                pe.wait_ge(ones_row, 2)
                for part in range(QUADS + 2):
                    slot = pre(0, part // QUADS, part % QUADS, part)
                    slot(0)
                    slot(1)
                    if part == QUADS - 1:
                        row(0, 0)

                head(0, 0, True, 2)
                head(0, 1, False, 2)
                with pe.Fori(1, LASTPAIR) as i:
                    head(i, 0, False, 2)
                    head(i, 1, False, 2)
                head(LASTPAIR, 0, False, 1)
                head(LASTPAIR, 1, False, 0)
                weighted(LASTPAIR, 1, QUADS - 1)
                denominator(LASTPAIR, 1)
                output(LASTPAIR, 1)

            @block.scalar
            def _(act):
                def copy_row(i, s):
                    h = 2 * i + s
                    act.wait_ge(row_ready, h + 1)
                    nc.scalar.activation(q_stack[KROWS:KROWS + 1, h, :], misc_ps[KROWS:KROWS + 1, :],
                                         ACT.Copy).then_inc(row_set, 1)

                def read_pv(i, s):
                    h = 2 * i + s
                    act.wait_ge(pv_done, QUADS * (h + 1))
                    wait(act, o_ready, h - 1)
                    nc.scalar.activation(pv_sum[:, s], pv_ps[:], ACT.Copy).then_inc(pv_read, 1)

                def head(i, s, first, last):
                    before = (i, 0) if s else (i - 1, 1)
                    after = (i, 1) if s == 0 else (i + 1, 0)
                    for q in range(QUADS):
                        Q = quad_no(i, s, q)
                        wait(act, pv_done, Q + 1 - PSLOTS)
                        wait(act, dve_summed, Q + 1 - PSLOTS)
                        wait(act, pool_summed, Q + 1 - PSLOTS)
                        for t in range(BT):
                            act.wait_ge(s_ready, BT * Q + t + 1)
                            nc.scalar.activation(prob[:, q % PSLOTS, t, :], s_ps[:, t % 2], ACT.Exp,
                                                 scale=SCALE).then_inc(p_ready, 1)
                        if q == 0 and not first:
                            read_pv(*before)
                        if q == QUADS - 2 and last >= 1:
                            copy_row(*after)

                copy_row(0, 0)
                head(0, 0, True, 2)
                head(0, 1, False, 2)
                with act.Fori(1, LASTPAIR) as i:
                    head(i, 0, False, 2)
                    head(i, 1, False, 2)
                head(LASTPAIR, 0, False, 1)
                head(LASTPAIR, 1, False, 0)
                read_pv(LASTPAIR, 1)

            @block.vector
            def _(dve):
                nc.vector.memset(k_stack[KROWS:KROWS + 1, 0, :], 1.0).then_inc(ones_row, 1)
                nc.vector.memset(k_stack[KROWS:KROWS + 1, 1, :], 1.0).then_inc(ones_row, 1)

                def pre_max(s, part, seen):
                    c = part // 2
                    for b in range(2):
                        tt = 2 * (part % 2) + b
                        dve.wait_ge(pre_ready, seen * 2 + b + 1)
                        nc.vector.tensor_reduce(part_max[:, s, tt, c:c + 1], pre_ps[:, b], AX.XY,
                                                ALU.max).then_inc(pre_read, 1)

                def head_max(h, s):
                    dve.wait_ge(pre_read, 2 * QUADS * (h + 1))
                    wait(dve, row_ready, h - 1)
                    nc.vector.tensor_reduce(neg_max[:, s], part_max[:, s], AX.X, ALU.max,
                                            negate=True).then_inc(max_ready, 1)

                def add_up(i, s, q):
                    Q = quad_no(i, s, q)
                    if q:
                        dve.wait_ge(p_ready, BT * Q + 2)
                    if q == 1:
                        wait(dve, den_ready, 2 * i + s - 1)
                        nc.vector.tensor_tensor(sum_dve[:, s], prob[:, 0, 0:2], prob[:, 1, 0:2],
                                                ALU.add).then_inc(dve_summed, 2)
                    elif q > 1:
                        dve.wait_ge(dve_summed, Q)
                        nc.vector.tensor_tensor(sum_dve[:, s], sum_dve[:, s], prob[:, q % PSLOTS, 0:2],
                                                ALU.add).then_inc(dve_summed, 1)

                def invert(i, s):
                    dve.wait_ge(den_ready, 2 * i + s + 1)
                    nc.vector.reciprocal(recip[:], misc_ps[:, 0:P]).then_inc(recip_ready, 1)

                def scale_out(i, s):
                    h = 2 * i + s
                    dve.wait_ge(recip_ready, h + 1)
                    dve.wait_ge(o_ready, h + 1)
                    wait(dve, o_stored[s], 16 * TT * i)
                    nc.vector.tensor_tensor(o_out[:, s], misc_ps[:, 0:P], recip[:], ALU.mult).then_inc(o_scaled, 1)

                def head(i, s, first, last):
                    h = 2 * i + s
                    before = (i, 0) if s else (i - 1, 1)
                    for q in range(QUADS):
                        if q < QUADS - 2:
                            if last >= 1:
                                pre_max(1 - s, q + 2, QUADS * (h + 1) + q + 2)
                            if q == QUADS - 3 and last >= 1:
                                head_max(h + 1, 1 - s)
                        elif last >= 2:
                            pre_max(s, q - (QUADS - 2), QUADS * (h + 1) + q + 2)
                        add_up(i, s, q)
                        if q == 2 and not first:
                            invert(*before)
                        if q == 5 and not first:
                            scale_out(*before)

                for part in range(QUADS + 2):
                    pre_max(part // QUADS, part % QUADS, part)
                    if part == QUADS - 1:
                        head_max(0, 0)
                head(0, 0, True, 2)
                head(0, 1, False, 2)
                with dve.Fori(1, LASTPAIR) as i:
                    head(i, 0, False, 2)
                    head(i, 1, False, 2)
                head(LASTPAIR, 0, False, 1)
                head(LASTPAIR, 1, False, 0)
                invert(LASTPAIR, 1)
                scale_out(LASTPAIR, 1)

            @block.gpsimd
            def _(pool):
                def add_up(i, s, q):
                    Q = quad_no(i, s, q)
                    if q:
                        pool.wait_ge(p_ready, BT * (Q + 1))
                    if q == 1:
                        wait(pool, den_ready, 2 * i + s - 1)
                        nc.gpsimd.tensor_tensor(sum_pool[:, s], prob[:, 0, 2:4], prob[:, 1, 2:4],
                                                ALU.add).then_inc(pool_summed, 2)
                    elif q > 1:
                        pool.wait_ge(pool_summed, Q)
                        nc.gpsimd.tensor_tensor(sum_pool[:, s], sum_pool[:, s], prob[:, q % PSLOTS, 2:4],
                                                ALU.add).then_inc(pool_summed, 1)

                for s in range(2):
                    for q in range(QUADS):
                        add_up(0, s, q)
                with pool.Fori(1, H // 2) as i:
                    for s in range(2):
                        for q in range(QUADS):
                            add_up(i, s, q)

        attend_stack.close()

        with ExitStack() as st:
            stage = "mlp_"
            sb, ps, sem = sb_in(st, stage), ps_in(st, stage), sem_in(st, stage)
            w1 = sb("w1", [P, DK, FF])
            w2 = sb("w2", [P, FM, D])
            b1 = sb("b1", [P, FM])
            oT = sb("oT", [P, DK, T])
            hT = sb("hT", [P, FM, T])
            h_ps = ps("h_ps", [P, 4, T])
            y_ps = ps("y_ps", [P, TT, D])
            o_in = sem("o_in")
            w1_in = sem("w1_in")
            w2_in = sem("w2_in")
            h_ready = sem("h_ready")
            h_read = sem("h_read")
            y_ready = sem("y_ready")
            y_added = sem("y_added")
            block = st.enter_context(nc.Block())

            @block.sync
            def _(sp):
                sp.dma_start(oT[:], o_dram[:].rearrange("(k p) t -> p k t", p=P)).then_inc(o_in, 16)
                sp.dma_start(w1[:], a["L0_xattn_W1"].rearrange("(k p) n -> p k n", p=P)).then_inc(w1_in, 16)
                with nc.allow_non_contiguous_dma(reason="biases, one to a partition"):
                    sp.dma_start(b1[:], a["L0_xattn_b1"].rearrange("(m p) -> p m", p=P)).then_inc(w1_in, 16)
                sp.dma_start(w2[:], a["L0_xattn_W2"].rearrange("(k p) n -> p k n", p=P)).then_inc(w2_in, 16)

            @block.tensor
            def _(pe):
                pe.wait_ge(o_in, 16)
                pe.wait_ge(w1_in, 32)
                for m in range(FM):
                    wait(pe, h_read, m - 3)
                    for k in range(DK):
                        last = nc.tensor.matmul(h_ps[:, m % 4], w1[:, k, m * P:(m + 1) * P], oT[:, k],
                                                start=k == 0, stop=k == DK - 1)
                    last.then_inc(h_ready, 1)
                pe.wait_ge(w2_in, 16)
                pe.wait_ge(h_read, FM)
                for t in range(TT):
                    for k in range(FM):
                        last = nc.tensor.matmul(y_ps[:, t], hT[:, k, t * P:(t + 1) * P], w2[:, k],
                                                start=k == 0, stop=k == FM - 1)
                    last.then_inc(y_ready, 1)

            @block.scalar
            def _(act):
                act.wait_ge(w1_in, 32)
                for m in range(FM):
                    act.wait_ge(h_ready, m + 1)
                    nc.scalar.activation(hT[:, m], h_ps[:, m % 4], ACT.Relu, bias=b1[:, m:m + 1]).then_inc(h_read, 1)

            @block.vector
            def _(dve):
                for t in range(TT):
                    dve.wait_ge(y_ready, t + 1)
                    nc.vector.tensor_tensor(x[:, t], x[:, t], y_ps[:, t], ALU.add).then_inc(y_added, 1)
                dve.wait_ge(y_added, TT)

        with ExitStack() as st:
            stage = "local_"
            sb, ps, sem = sb_in(st, stage), ps_in(st, stage), sem_in(st, stage)
            wqkv = sb("wqkv", [P, DK, 3 * D])
            wout = sb("wout", [P, DK, D])
            cos = sb("cos", [P, T])
            sin = sb("sin", [P, T])
            rot = sb("rot", [P, P])
            mask = sb("mask", [P, 2 * P])
            maskb = sb("maskb", [P, 2 * P], BF16)
            identb = sb("identb", [P, P], BF16)
            xn = sb("xn", [P, TT, D])
            xnT = sb("xnT", [P, DK, T])
            qk = sb("qk", [P, 2, T])
            t_cos = sb("t_cos", [P, T])
            t_sin = sb("t_sin", [P, T])
            q_pad = sb("q_pad", [P, H, T])
            kT = sb("kT", [P, G, T])
            v = sb("v_local", [P, TT, D])
            HU = 2
            KW = 3 * P
            top = sb("top", [P, 2, HU])
            bias = sb("bias", [P, 2, HU])
            total = sb("total", [P, 2, HU])
            inv = sb("inv", [P, 2, HU])
            pr = sb("pr", [P, 2, HU, KW])
            prT = sb("prT", [P, 2, HU, KW])
            oT = sb("oT_local", [P, G, T])
            s_ps = ps("sl_ps", [P, 2, HU, D])
            t_ps = ps("t_ps", [P, HU, D])
            o_ps = ps("ol_ps", [P, 2, D])

            w_in_l = sem("w_in_l")
            const_in = sem("const_in")
            consts = sem("consts")
            padded = sem("padded")
            turned = sem("turned_l")
            turned_out = sem("turned_out_l")
            qk_ready = sem("qk_ready")
            qk_out = sem("qk_out")
            rot_ready = sem("rot_ready")
            t_ready = sem("t_ready")
            roped = sem("roped")
            v_ready = sem("v_ready_l")
            v_read = sem("v_read_l")
            s_ready = sem("s_ready_l")
            top_ready = sem("top_ready")
            bias_ready = sem("bias_ready")
            p_ready = sem("p_ready_l")
            inv_ready = sem("inv_ready")
            p_scaled = sem("p_scaled")
            pT_ready = sem("pT_ready")
            pT_read = sem("pT_read")
            o_ready = sem("o_ready_l")
            o_read = sem("o_read_l")
            y_ready = sem("y_ready_l")
            y_added = sem("y_added_l")
            dve_chain = sem("dve_chain_l")
            seen = [(max(0, t - WINDOW // P), min(t, WINDOW // P) + 1) for t in range(TT)]
            units = [(g, t, hu) for g in range(G) for t in range(TT) for hu in range(HG // HU)]
            block = st.enter_context(nc.Block())

            @block.sync
            def _(sp):
                for dst, n in ((cos, "c_cos"), (sin, "c_sin"), (rot, "c_rot"), (mask, "c_mask")):
                    sp.dma_start(dst[:], a[n]).then_inc(const_in, 16)
                sp.dma_start(wqkv[:], a["L0_attn_Wqkv"].rearrange("(k p) n -> p k n", p=P)).then_inc(w_in_l, 16)
                sp.dma_start(wout[:], a["L0_attn_Wout"].rearrange("(k p) n -> p k n", p=P)).then_inc(w_in_l, 16)

            @block.gpsimd
            def _(pool):
                nc.gpsimd.memset(q_pad[:], 0.0).then_inc(padded, 1)
                pool.wait_ge(const_in, 64)
                nc.gpsimd.tensor_copy(maskb[:], mask[:]).then_inc(consts, 1)
                nc.gpsimd.tensor_copy(identb[:], ident[:]).then_inc(consts, 1)

            @block.scalar
            def _(act):
                layer_norm_scalar(act, var_ready, sd_ready, 2)
                for m in range(2 * G):
                    act.wait_ge(qk_ready, m + 1)
                    wait(act, roped, m - 1)
                    nc.scalar.activation(qk[:, m % 2], s_ps[:, 0, m % 2], ACT.Copy).then_inc(qk_out, 1)
                for t in range(TT):
                    act.wait_ge(v_ready, t + 1)
                    nc.scalar.activation(v[:, t], t_ps[:, t % 2], ACT.Copy).then_inc(v_read, 1)

                def turn_out(n):
                    g, t, hu = units[n]
                    w = seen[t][1] * P
                    act.wait_ge(pT_ready, n + 1)
                    wait(act, o_ready, n - 1)
                    nc.scalar.activation(prT[:, n % 2, :, 0:w], t_ps[:, :, 0:w], ACT.Copy).then_inc(pT_read, 1)

                for n, (g, t, hu) in enumerate(units):
                    w = seen[t][1] * P
                    act.wait_ge(bias_ready, n + 1)
                    wait(act, pT_ready, n - 1)
                    for j in range(HU):
                        last = nc.scalar.activation(pr[:, n % 2, j, 0:w], s_ps[:, n % 2, j, 0:w], ACT.Exp,
                                                    bias=bias[:, n % 2, j:j + 1], scale=SCALE,
                                                    accum_out=total[:, n % 2, j:j + 1])
                        last.then_inc(p_ready, 1)
                    if n >= 1:
                        turn_out(n - 1)
                turn_out(len(units) - 1)

            @block.vector
            def _(dve):
                chain = Chain(dve, dve_chain)
                layer_norm_vector(dve, chain, var_ready, sd_ready, 2, xn, xn_ready)
                for k in range(DK):
                    dve.wait_ge(turned, k + 1)
                    nc.vector.tensor_copy(xnT[:, k], s_ps[:, 1, k % 2]).then_inc(turned_out, 1)
                dve.wait_ge(const_in, 64)
                dve.wait_ge(padded, 1)
                for m in range(2 * G):
                    dve.wait_ge(qk_out, m + 1)
                    chain.wait()
                    wait(dve, roped, m)
                    chain(nc.vector.tensor_tensor(t_cos[:], qk[:, m % 2], cos[:], ALU.mult))
                    dve.wait_ge(rot_ready, m + 1)
                    chain.link(nc.vector.tensor_tensor(t_sin[:], s_ps[:, 1, m % 2], sin[:], ALU.mult))
                    if m < G:
                        for i in range(HG):
                            rows = slice(i * HD, (i + 1) * HD)
                            last = nc.vector.tensor_tensor(q_pad[rows, m * HG + i], t_cos[rows], t_sin[rows], ALU.add)
                            if i < HG - 1:
                                chain(last)
                        last.then_inc(roped, 1)
                    else:
                        nc.vector.tensor_tensor(kT[:, m - G], t_cos[:], t_sin[:], ALU.add).then_inc(roped, 1)

                def normalise(n):
                    g, t, hu = units[n]
                    w = seen[t][1] * P
                    dve.wait_ge(p_ready, HU * (n + 1))
                    nc.vector.reciprocal(inv[:, n % 2], total[:, n % 2]).then_inc(inv_ready, 1)
                    dve.wait_ge(inv_ready, n + 1)
                    for j in range(HU):
                        nc.vector.tensor_scalar(pr[:, n % 2, j, 0:w], pr[:, n % 2, j, 0:w], inv[:, n % 2, j:j + 1],
                                                None, ALU.mult).then_inc(p_scaled, 1)

                def out_copy(g, t):
                    dve.wait_ge(o_ready, HG // HU * (g * TT + t + 1))
                    nc.vector.tensor_copy(oT[:, g, t * P:(t + 1) * P],
                                          o_ps[:, t % 2, 0:P]).then_inc(o_read, 1)

                for n, (g, t, hu) in enumerate(units):
                    w = seen[t][1] * P
                    dve.wait_ge(s_ready, n + 1)
                    nc.vector.tensor_reduce(top[:, n % 2], s_ps[:, n % 2, :, 0:w], AX.X, ALU.max,
                                            negate=True).then_inc(top_ready, 1)
                    dve.wait_ge(top_ready, n + 1)
                    wait(dve, p_ready, HU * (n - 1))
                    nc.vector.tensor_scalar(bias[:, n % 2], top[:, n % 2], SCALE, None, ALU.mult).then_inc(bias_ready, 1)
                    if n >= 1:
                        normalise(n - 1)
                    if n >= 3 and units[n - 3][2] == HG // HU - 1:
                        out_copy(*units[n - 3][:2])
                normalise(len(units) - 1)
                done = [u for n, u in enumerate(units) if n < len(units) - 3 and u[2] == HG // HU - 1]
                for g in range(G):
                    for t in range(TT):
                        if (g, t, HG // HU - 1) not in done:
                            out_copy(g, t)
                for t in range(TT):
                    dve.wait_ge(y_ready, t + 1)
                    nc.vector.tensor_tensor(x[:, t], x[:, t], s_ps[:, t // 2, t % 2], ALU.add).then_inc(y_added, 1)
                dve.wait_ge(y_added, TT)

            @block.tensor
            def _(pe):
                pe.wait_ge(xn_ready, 2 * TT)
                for k in range(DK):
                    wait(pe, turned_out, k - 1)
                    for t in range(TT):
                        last = nc.tensor.transpose(s_ps[:, 1, k % 2, t * P:(t + 1) * P], xn[:, t, k * P:(k + 1) * P],
                                                   ident[:])
                    last.then_inc(turned, 1)
                pe.wait_ge(turned_out, DK)
                pe.wait_ge(w_in_l, 32)
                pe.wait_ge(const_in, 64)

                def rotate(m):
                    pe.wait_ge(qk_out, m + 1)
                    wait(pe, roped, m - 1)
                    nc.tensor.matmul(s_ps[:, 1, m % 2], rot[:], qk[:, m % 2], start=True, stop=True).then_inc(rot_ready, 1)

                for m in range(2 * G):
                    wait(pe, qk_out, m - 1)
                    for k in range(DK):
                        last = nc.tensor.matmul(s_ps[:, 0, m % 2], wqkv[:, k, m * P:(m + 1) * P], xnT[:, k],
                                                start=k == 0, stop=k == DK - 1)
                    last.then_inc(qk_ready, 1)
                    if m >= 1:
                        rotate(m - 1)
                rotate(2 * G - 1)
                for t in range(TT):
                    wait(pe, v_read, t - 1)
                    for k in range(DK):
                        last = nc.tensor.matmul(t_ps[:, t % 2], xnT[:, k, t * P:(t + 1) * P], wqkv[:, k, 2 * D:3 * D],
                                                start=k == 0, stop=k == DK - 1)
                    last.then_inc(v_ready, 1)
                pe.wait_ge(v_read, TT)
                pe.wait_ge(roped, 2 * G)
                pe.wait_ge(consts, 2)

                def local_scores(n):
                    g, t, hu = units[n]
                    k0, nk = seen[t]
                    wait(pe, p_ready, HU * (n - 1))
                    for j in range(HU):
                        head = g * HG + hu * HU + j
                        nc.tensor.matmul(s_ps[:, n % 2, j, 0:nk * P], q_pad[:, head, t * P:(t + 1) * P],
                                         kT[:, g, k0 * P:(k0 + nk) * P], start=True, stop=False)
                        if t >= WINDOW // P:
                            nc.tensor.matmul(s_ps[:, n % 2, j, 0:P], identb[:], maskb[:, P:2 * P], start=False, stop=False)
                        last = nc.tensor.matmul(s_ps[:, n % 2, j, (nk - 1) * P:nk * P], identb[:], maskb[:, 0:P],
                                                start=False, stop=True)
                    last.then_inc(s_ready, 1)

                def turn(n):
                    g, t, hu = units[n]
                    pe.wait_ge(p_scaled, HU * (n + 1))
                    wait(pe, pT_read, n)
                    for j in range(HU):
                        for k in range(seen[t][1]):
                            last = nc.tensor.transpose(t_ps[:, j, k * P:(k + 1) * P], pr[:, n % 2, j, k * P:(k + 1) * P],
                                                       ident[:])
                    last.then_inc(pT_ready, 1)

                def values(n):
                    g, t, hu = units[n]
                    k0, nk = seen[t]
                    pe.wait_ge(pT_read, n + 1)
                    if hu == 0:
                        wait(pe, o_read, g * TT + t - 1)
                    for k in range(nk):
                        for j in range(HU):
                            head = g * HG + hu * HU + j
                            r = (hu * HU + j) * HD
                            last = nc.tensor.matmul(o_ps[r:r + HD, t % 2, 0:P], v[:, k0 + k, head * HD:(head + 1) * HD],
                                                    prT[:, n % 2, j, k * P:(k + 1) * P], start=k == 0, stop=k == nk - 1)
                    last.then_inc(o_ready, 1)

                for n in range(len(units)):
                    local_scores(n)
                    if n >= 1:
                        turn(n - 1)
                    if n >= 2:
                        values(n - 2)
                turn(len(units) - 1)
                values(len(units) - 2)
                values(len(units) - 1)
                pe.wait_ge(o_read, G * TT)
                pe.wait_ge(p_ready, HU * len(units))
                for t in range(TT):
                    for k in range(DK):
                        last = nc.tensor.matmul(s_ps[:, t // 2, t % 2], oT[:, k, t * P:(t + 1) * P], wout[:, k],
                                                start=k == 0, stop=k == DK - 1)
                    last.then_inc(y_ready, 1)

        with ExitStack() as st:
            stage = "ffn_"
            sb, ps, sem = sb_in(st, stage), ps_in(st, stage), sem_in(st, stage)
            row_g = [sb(f"row_w{s}", [P, D]) for s in range(4)]
            wT = [sb("wgT", [P, DK, INNER]), sb("wuT", [P, DK, INNER])]
            wdT = sb("wdT", [P, IK, D])
            xn = sb("xn_f", [P, D * TT])
            xq = sb("xq", [P, D * TT])
            xqT = sb("xqT", [P, DK, T])
            hT = sb("hqT", [P, IK, P])
            h = sb("h", [P, 1, INNER])
            hq = sb("hq", [P, INNER])
            e = sb("e", [P, 512])
            gate = sb("gate", [P, 512])
            NQ = max(D * TT // 2, INNER)
            amax = sb("amax_f", [P, NQ // QB])
            qscale = sb("qscale_f", [P, NQ // QB])
            qinv = sb("qinv_f", [P, NQ // QB])
            qn = sb("qn_f", [P, NQ])
            qa = sb("qa_f", [P, NQ])
            q1 = sb("q1_f", [P, NQ])
            q2 = sb("q2_f", [P, NQ])
            w_ps = ps("w_ps", [P, 2, D])
            g_ps = ps("g_ps", [P, 2, D])
            u_ps = ps("u_ps", [P, 2, D])
            y_ps = ps("yf_ps", [P, 2, D])

            row_in = [sem(f"row_in{s}") for s in range(4)]
            w_turned = sem("w_turned")
            w_out = sem("w_out_f")
            xq_ready = sem("xq_ready")
            x_turned = sem("x_turned")
            x_out = sem("x_out")
            gate_ready = sem("gate_ready")
            e_ready = sem("e_ready")
            gu_read = sem("gu_read")
            hq_ready = sem("hq_ready")
            h_turned = sem("h_turned")
            h_out = sem("h_out")
            y_ready = sem("y_ready_f")
            y_added = sem("y_added_f")
            stored = sem("stored")
            dve_chain = sem("dve_chain_f")

            gate_rows = [wq_dram[w][:].rearrange("p (r c) -> (p r) c", c=D).rearrange("(m p) c -> m p c", p=P) for w in range(2)]
            down_rows = wq_dram[2][:].rearrange("p (r c) -> (p r) c", c=INNER).rearrange("(n p) c -> p n c", p=P)
            rows = [(w, m) for m in range(IK) for w in range(2)] + [(2, m) for m in range(IK)]
            cuts = [(0, 512), (512, 1024), (1024, INNER)]
            block = st.enter_context(nc.Block())

            @block.sync
            def _(sp):
                for n, (w, m) in enumerate(rows):
                    wait(sp, w_turned, n - 3)
                    if w < 2:
                        sp.dma_start(row_g[n % 4][:], gate_rows[w][m]).then_inc(row_in[n % 4], 16)
                    else:
                        sp.dma_start(row_g[n % 4][:].rearrange("p (n c) -> p n c", c=P),
                                     down_rows[:, :, m * P:(m + 1) * P]).then_inc(row_in[n % 4], 16)
                for t in range(TT):
                    sp.wait_ge(y_added, t + 1)
                    sp.dma_start(out[0, t * P:(t + 1) * P, :], x[:, t]).then_inc(stored, 16)
                sp.wait_ge(stored, 16 * TT)

            @block.scalar
            def _(act):
                layer_norm_scalar(act, var_ready, sd_ready, 3)
                for n, (w, m) in enumerate(rows):
                    act.wait_ge(w_turned, n + 1)
                    if w < 2:
                        dst = wT[w][:, :, m * P:(m + 1) * P]
                        src = w_ps[:, n % 2].rearrange("p (k c) -> p k c", c=P)
                    else:
                        dst, src = wdT[:, m], w_ps[:, n % 2]
                    nc.scalar.activation(dst, src, ACT.Copy).then_inc(w_out, 1)
                n = 0
                for t in range(TT):
                    for lo, hi in cuts:
                        act.wait_ge(gate_ready, n + 1)
                        wait(act, gu_read, n)
                        nc.scalar.activation(e[:, 0:hi - lo], g_ps[:, n % 2, 0:hi - lo], ACT.Exp, scale=-1.0).then_inc(e_ready, 1)
                        n += 1

            @block.vector
            def _(dve):
                chain = Chain(dve, dve_chain)

                def quantize(src, dst, n, ready):
                    def blocks(ap):
                        return ap.rearrange("p (b e) -> p b e", e=QB)
                    nb = n // QB
                    def each(s):
                        return s[:, 0:nb].unsqueeze(2).to_broadcast([P, nb, QB])
                    chain.link(nc.vector.tensor_reduce(amax[:, 0:nb], blocks(src), AX.X, ALU.max, apply_absolute_value=True))
                    chain.link(nc.vector.tensor_scalar(qscale[:, 0:nb], amax[:, 0:nb], 1.0 / 6.0, 1e-12, ALU.mult, ALU.max))
                    chain.link(nc.vector.reciprocal(qinv[:, 0:nb], qscale[:, 0:nb]))
                    chain.link(nc.vector.tensor_scalar(qinv[:, 0:nb], qinv[:, 0:nb], BELOW, None, ALU.mult))
                    chain.link(nc.vector.tensor_tensor(blocks(qn[:, 0:n]), blocks(src), each(qinv), ALU.mult))
                    chain.link(nc.vector.tensor_scalar(qa[:, 0:n].bitcast(U32), qn[:, 0:n].bitcast(U32), 0x7FFFFFFF, None,
                                                       ALU.bitwise_and))
                    chain(nc.vector.tensor_scalar(q1[:, 0:n], qa[:, 0:n], 2.0, ROUND[0.5], ALU.min, ALU.add))
                    chain.link(nc.vector.tensor_scalar(q2[:, 0:n], qa[:, 0:n], 2.0, 4.0, ALU.max, ALU.min))
                    chain.link(nc.vector.tensor_scalar(q2[:, 0:n], q2[:, 0:n], ROUND[1.0], -ROUND[1.0], ALU.add, ALU.add))
                    chain(nc.vector.tensor_scalar(qa[:, 0:n], qa[:, 0:n], 4.0, ROUND[2.0], ALU.max, ALU.add))
                    chain.link(nc.vector.scalar_tensor_tensor(out=q1[:, 0:n], in0=q1[:, 0:n], scalar=ROUND[0.5],
                                                              in1=q2[:, 0:n], op0=ALU.subtract, op1=ALU.add))
                    chain.link(nc.vector.scalar_tensor_tensor(out=q1[:, 0:n], in0=qa[:, 0:n], scalar=ROUND[2.0] + 6.0,
                                                              in1=q1[:, 0:n], op0=ALU.subtract, op1=ALU.add))
                    chain.link(nc.vector.scalar_tensor_tensor(out=q1[:, 0:n].bitcast(U32), in0=qn[:, 0:n].bitcast(U32),
                                                              scalar=0x80000000, in1=q1[:, 0:n].bitcast(U32),
                                                              op0=ALU.bitwise_and, op1=ALU.bitwise_or))
                    nc.vector.tensor_tensor(blocks(dst), blocks(q1[:, 0:n]), each(qscale), ALU.mult).then_inc(ready, 1)

                xn_t = xn[:].rearrange("p (t d) -> p t d", t=TT)
                layer_norm_vector(dve, chain, var_ready, sd_ready, 3, xn_t, xn_ready)
                dve.wait_ge(xn_ready, 3 * TT)
                half = D * TT // 2
                for s in range(2):
                    wait(dve, xq_ready, s)
                    quantize(xn[:, s * half:(s + 1) * half], xq[:, s * half:(s + 1) * half], half, xq_ready)
                for k in range(DK):
                    dve.wait_ge(x_turned, k + 1)
                    nc.vector.tensor_copy(xqT[:, k], y_ps[:, k % 2]).then_inc(x_out, 1)

                def turned_out(t):
                    for c in range(3):
                        w = min(4, IK - 4 * c) * P
                        dve.wait_ge(h_turned, 3 * t + c + 1)
                        nc.vector.tensor_copy(hT[:, 4 * c:4 * c + w // P].rearrange("p k c -> p (k c)"),
                                              w_ps[:, c % 2, 0:w]).then_inc(h_out, 1)

                def add_out(t):
                    dve.wait_ge(y_ready, t + 1)
                    nc.vector.tensor_tensor(x[:, t], x[:, t], y_ps[:, t % 2], ALU.add).then_inc(y_added, 1)

                n = 0
                for t in range(TT):
                    for lo, hi in cuts:
                        w = hi - lo
                        dve.wait_ge(e_ready, n + 1)
                        chain.link(nc.vector.tensor_scalar(gate[:, 0:w], e[:, 0:w], 1.0, None, ALU.add))
                        chain.link(nc.vector.reciprocal(gate[:, 0:w], gate[:, 0:w]))
                        chain.link(nc.vector.tensor_tensor(gate[:, 0:w], gate[:, 0:w], g_ps[:, n % 2, 0:w], ALU.mult))
                        nc.vector.tensor_tensor(h[:, 0, lo:hi], gate[:, 0:w], u_ps[:, n % 2, 0:w], ALU.mult).then_inc(gu_read, 1)
                        n += 1
                    if t >= 1:
                        wait(dve, y_ready, t - 1)
                        turned_out(t - 1)
                    if t >= 2:
                        add_out(t - 2)
                    dve.wait_ge(gu_read, n)
                    wait(dve, h_turned, 3 * t)
                    quantize(h[:, 0, :], hq[:], INNER, hq_ready)
                dve.wait_ge(y_ready, TT - 1)
                turned_out(TT - 1)
                add_out(TT - 2)
                add_out(TT - 1)

            @block.tensor
            def _(pe):
                for n, (w, m) in enumerate(rows):
                    pe.wait_ge(row_in[n % 4], 16 * (n // 4 + 1))
                    wait(pe, w_out, n - 1)
                    for k in range(DK):
                        last = nc.tensor.transpose(w_ps[:, n % 2, k * P:(k + 1) * P], row_g[n % 4][:, k * P:(k + 1) * P],
                                                   ident[:])
                    last.then_inc(w_turned, 1)
                pe.wait_ge(xq_ready, 2)
                xq_t = xq[:].rearrange("p (t d) -> p t d", t=TT)
                for k in range(DK):
                    wait(pe, x_out, k - 1)
                    for t in range(TT):
                        last = nc.tensor.transpose(y_ps[:, k % 2, t * P:(t + 1) * P], xq_t[:, t, k * P:(k + 1) * P], ident[:])
                    last.then_inc(x_turned, 1)
                pe.wait_ge(x_out, DK)
                pe.wait_ge(w_out, len(rows))

                def gate_up(t):
                    for c, (lo, hi) in enumerate(cuts):
                        n = 3 * t + c
                        wait(pe, gu_read, n - 1)
                        for bank, wt in ((g_ps, wT[0]), (u_ps, wT[1])):
                            for k in range(DK):
                                last = nc.tensor.matmul(bank[:, n % 2, 0:hi - lo], xqT[:, k, t * P:(t + 1) * P], wt[:, k, lo:hi],
                                                        start=k == 0, stop=k == DK - 1)
                        last.then_inc(gate_ready, 1)

                def down(t):
                    pe.wait_ge(hq_ready, t + 1)
                    for c in range(3):
                        wait(pe, h_out, 3 * t + (c == 2))
                        for k in range(4 * c, min(4 * c + 4, IK)):
                            last = nc.tensor.transpose(w_ps[:, c % 2, (k - 4 * c) * P:(k - 4 * c + 1) * P],
                                                       hq[:, k * P:(k + 1) * P], ident[:])
                        last.then_inc(h_turned, 1)
                    pe.wait_ge(h_out, 3 * (t + 1))
                    wait(pe, y_added, t - 1)
                    for k in range(IK):
                        last = nc.tensor.matmul(y_ps[:, t % 2], hT[:, k], wdT[:, k], start=k == 0, stop=k == IK - 1)
                    last.then_inc(y_ready, 1)

                for t in range(TT):
                    gate_up(t)
                    if t >= 1:
                        down(t - 1)
                down(TT - 1)


_INS = ["x", "ctx_768", "L0_xattn_Wq", "L0_xattn_bq", "L0_xattn_Wk", "L0_xattn_bk", "L0_xattn_Wv", "L0_xattn_bv",
        "L0_xattn_W1", "L0_xattn_b1", "L0_xattn_W2", "L0_xattn_b2", "L0_attn_Wqkv", "L0_attn_Wout",
        "L0_ffn_w_gate", "L0_ffn_w_up", "L0_ffn_w_down"]


def kernel(**inputs):
    import numpy as _np
    import concourse.bacc as _bacc
    from concourse import mybir as _mybir
    from concourse.bass_utils import run_bass_kernel_spmd as _run

    nc = _bacc.Bacc("TRN2", target_bir_lowering=False, num_devices=1)
    named = {n: _np.ascontiguousarray(inputs[n]) for n in _INS}
    named.update({"c_" + n: c for n, c in constants().items()})
    arrays, args = {}, {}
    for name, array in named.items():
        arrays[f"in_{name}_dram"] = array
        args[name] = nc.dram_tensor(f"in_{name}_dram", array.shape, _mybir.dt.from_np(array.dtype),
                                    kind="ExternalInput").ap()
    out = nc.dram_tensor("out_0_dram", (1, T, D), _mybir.dt.float32, kind="ExternalOutput").ap()
    perceiver(nc, args, out)
    r = _run(nc, [arrays], core_ids=[0])
    return r.results[0]["out_0_dram"]
```

```python
from contextlib import ExitStack

import numpy as np

import concourse.bass as bass
from concourse import mybir

ALU = mybir.AluOpType
ACT = mybir.ActivationFunctionType
AX = mybir.AxisListType
F32 = mybir.dt.float32
F16 = mybir.dt.float16
BF16 = mybir.dt.bfloat16
U32 = mybir.dt.uint32

P = 128
T = 512
D = 512
TT = T // P
DK = D // P
M = 8192
C = 384
CK = C // P
H = 16
HD = D // H
G = 4
HG = H // G
BLK = 512
NB = M // BLK
BT = BLK // P
FF = 2 * D
FM = FF // P
INNER = 1408
IK = INNER // P
WINDOW = 256
QB = 16
WSCALE = 256.0
SCALE = float(HD) ** -0.5
EPS = 1e-5

QUADS = M // BLK
PSLOTS = 4
DSUM = 768
LAST_DSUM = 1280
CH = 4
CHK = M // CH
KROWS = 3 * HD

UN = INNER * D // P // (NB // 2)
EARLY = DK * 3 * D + DK * D + 2 * T + 3 * P
LATE = DK * FF + FM * D + FM + G

ROUND = {step: 1.5 * 2.0 ** 23 * step for step in (0.5, 1.0, 2.0)}
BELOW = 1.0 - 2.0 ** -23


class Chain:

    def __init__(self, eng, sem):
        self.eng, self.sem, self.n, self.moving = eng, sem, 0, 0

    def at(self, moving):
        self.moving = moving

    def __call__(self, ins):
        ins.then_inc(self.sem, 1)
        self.n += 1
        return ins

    def wait(self):
        self.eng.wait_ge(self.sem, self.n + self.moving)

    def link(self, ins):
        self(ins)
        self.wait()


def wait(eng, sem, value):
    if not (isinstance(value, int) and value <= 0):
        eng.wait_ge(sem, value)


def constants():
    half = HD // 2
    theta = (1.0 / np.float32(10000.0) ** (np.arange(half, dtype=np.float32) / np.float32(half))).astype(np.float32)
    freqs = np.arange(T, dtype=np.float32)[None, :] * np.tile(theta, 2 * HG)[:, None]
    rot = np.zeros((P, P), np.float32)
    for h in range(HG):
        for d in range(half):
            rot[h * HD + d + half, h * HD + d] = -1.0
            rot[h * HD + d, h * HD + d + half] = 1.0
    q, k = np.arange(P)[:, None], np.arange(P)[None, :]
    return {
        "cos": np.cos(freqs).astype(np.float32),
        "sin": np.sin(freqs).astype(np.float32),
        "rot": rot,
        "ident": np.eye(P, dtype=np.float32),
        "fold": np.tile(np.eye(HD, dtype=np.float32), (P // HD, 1)),
        "mask": np.concatenate([np.where(k <= q, 0.0, -1e30), np.where(k > q, 0.0, -1e30)], 1).astype(np.float32),
    }


def perceiver(nc, a, out):
    with ExitStack() as whole:
        def sb_in(stack, stage=""):
            return lambda name, shape, dt=F32: stack.enter_context(nc.sbuf_tensor(stage + name, shape, dt))

        def ps_in(stack, stage=""):
            return lambda name, shape, dt=F32: stack.enter_context(nc.psum_tensor(stage + name, shape, dt))

        def sem_in(stack, stage=""):
            return lambda name: stack.enter_context(nc.semaphore(stage + name))

        k_dram = nc.dram_tensor("k_scratch", [H, 2 * HD, M], F16)
        v_dram = nc.dram_tensor("v_scratch", [H, P, M // P, HD], F32)
        o_dram = nc.dram_tensor("o_scratch", [H * HD, T], F32)
        wq_dram = [nc.dram_tensor(f"fp4_{n}", [P, INNER * D // P], F32) for n in ("gate", "up", "down")]

        sb = sb_in(whole)
        x = sb("x", [P, TT, D])
        ident = sb("ident", [P, P])
        identh = sb("identh", [P, P], F16)
        ones = sb("ones", [P, HD])
        stats = sb("stats", [P, TT, 6])
        mv = sb("mv", [P, TT, 2])
        ve = sb("ve", [P, TT])
        sd = sb("sd", [P, TT])
        r0 = sb("r0", [P, TT])
        r1 = sb("r1", [P, TT])
        r2 = sb("r2", [P, TT])

        early = sb("early", [P, EARLY])
        late = sb("late", [P, LATE])

        def carve(area):
            at = [0]

            def piece(shape, dt=F32):
                size = int(np.prod(shape)) * (1 if dt == F32 else 0.5)
                size = int(size)
                ap = area[:, at[0]:at[0] + size]
                at[0] += size
                assert at[0] <= area.shape[1]
                if dt != F32:
                    ap = ap.bitcast(dt)
                names = "abcd"[:len(shape)]
                if len(shape) == 1:
                    return ap
                return ap.rearrange(f"p ({' '.join(names)}) -> p {' '.join(names)}", **dict(zip(names, shape)))
            return piece

        piece = carve(early)
        q_stack = piece([H, T], F16)
        y = piece([2, BT, C])
        w_in = piece([3, UN])
        piece = carve(late)
        wq = piece([DK, D])
        xn_q = piece([TT, D])
        xnT_q = piece([DK, T])
        qf = piece([G, T])

        def layer_norm_vector(dve, chain, var_ready, sd_ready, k, xn, xn_ready):
            for t in range(TT):
                chain(nc.vector.bn_stats(stats[:, t, :], x[:, t, :]))
            chain.wait()
            for t in range(TT):
                chain(nc.vector.bn_aggr(mv[:, t, :], stats[:, t, :]))
            chain.wait()
            nc.vector.tensor_scalar(ve[:], mv[:, :, 1], EPS, None, ALU.add).then_inc(var_ready, 1)
            dve.wait_ge(sd_ready, k)
            dve.wait_ge(var_ready, k)
            chain.link(nc.vector.reciprocal(r0[:], sd[:]))
            chain.link(nc.vector.tensor_tensor(r1[:], r0[:], r0[:], ALU.mult))
            chain.link(nc.vector.tensor_tensor(r2[:], r1[:], ve[:], ALU.mult))
            chain.link(nc.vector.tensor_scalar(r1[:], r2[:], -0.5, 1.5, ALU.mult, ALU.add))
            chain.link(nc.vector.tensor_tensor(r2[:], r0[:], r1[:], ALU.mult))
            for t in range(TT):
                nc.vector.tensor_scalar(xn[:, t, :], x[:, t, :], mv[:, t, 0:1], r2[:, t:t + 1],
                                        ALU.subtract, ALU.mult).then_inc(xn_ready, 1)

        def layer_norm_scalar(act, var_ready, sd_ready, k):
            act.wait_ge(var_ready, k)
            nc.scalar.activation(sd[:], ve[:], ACT.Sqrt).then_inc(sd_ready, 1)

        var_ready = sem_in(whole)("var_ready")
        sd_ready = sem_in(whole)("sd_ready")
        xn_ready = sem_in(whole)("xn_ready")

        with ExitStack() as st:
            stage = "project_"
            sb, ps, sem = sb_in(st, stage), ps_in(st, stage), sem_in(st, stage)
            wkv = sb("wkv", [P, 2, CK, D])
            w_hi = sb("w_hi", [P, 2, CK, D], F16)
            w_lo = sb("w_lo", [P, 2, CK, D], F16)
            bq = sb("bq", [P, G])
            bk = sb("bk", [P, G])
            b2 = sb("b2", [P, D])
            q_hi = sb("q_hi", [P, G, T], F16)
            q_lo = sb("q_lo", [P, G, T], F16)
            yT_hi = sb("yT_hi", [P, 2, CK, BLK], F16)
            yT_lo = sb("yT_lo", [P, 2, CK, BLK], F16)
            kf = sb("kf", [P, 2, BLK])
            k_hi = sb("k_hi", [P, 2, G, BLK], F16)
            k_lo = sb("k_lo", [P, 2, G, BLK], F16)
            v = sb("v", [P, 2, H, BT, HD])
            UB = UN // QB
            amax = sb("amax", [P, UB])
            qscale = sb("qscale", [P, UB])
            qinv = sb("qinv", [P, UB])
            qn = sb("qn", [P, UN])
            qa = sb("qa", [P, UN])
            q1 = sb("q1", [P, UN])
            q2 = sb("q2", [P, UN])
            q3 = sb("q3", [P, UN])
            w_out = sb("w_out", [P, 3, UN])

            yT_ps = ps("yT_ps", [P, CK, BLK])
            k_ps = ps("k_ps", [P, 2, BLK])
            v_ps = ps("v_ps", [P, 2, D])

            x_in = sem("x_in")
            cross_in = [sem(f"cross_in{w}") for w in range(2)]
            wq_in = sem("wq_in")
            b2_in = sem("b2_in")
            x_biased = sem("x_biased")
            bias_in = sem("bias_in")
            y_in = [sem(f"y_in{u}") for u in range(2)]
            w_unit_in = [sem(f"w_unit_in{w}") for w in range(3)]
            w_unit_out = [sem(f"w_unit_out{w}") for w in range(3)]
            const_ready = sem("const_ready")
            wsplit_hi = sem("wsplit_hi")
            wsplit_lo = sem("wsplit_lo")
            turned = sem("turned")
            turned_out = sem("turned_out")
            q_ready = sem("q_ready")
            qf_ready = sem("qf_ready")
            qhi_ready = sem("qhi_ready")
            qlo_ready = sem("qlo_ready")
            q_stacked = sem("q_stacked")
            yT_ready = sem("yT_ready")
            yhi_ready = sem("yhi_ready")
            ylo_ready = sem("ylo_ready")
            k_ready = sem("k_ready")
            khi_ready = sem("khi_ready")
            kf_ready = sem("kf_ready")
            klo_ready = sem("klo_ready")
            v_ready = sem("v_ready")
            vs_ready = sem("vs_ready")
            k_out = [sem(f"k_out{u}") for u in range(2)]
            v_out = [sem(f"v_out{u}") for u in range(2)]
            k_used = sem("k_used")
            v_used = sem("v_used")
            amax_done = sem("amax_done")
            qinv_ready = sem("qinv_ready")
            qn_ready = sem("qn_ready")
            q_done = sem("q_done")
            wq_ready = sem("wq_ready")
            dve_chain = sem("dve_chain_p")

            y_view = a["ctx_768"][0].rearrange("(b p t) c -> b p t c", p=P, t=BT)
            k_hi_view = k_dram[:, 0:HD, :].rearrange("(g i) d k -> i d g k", i=HG)
            k_lo_view = k_dram[:, HD:2 * HD, :].rearrange("(g i) d k -> i d g k", i=HG)
            v_view = v_dram[:].rearrange("h p t d -> p h (t d)")
            w_flat = [a[n].rearrange("(p r) c -> p (r c)", p=P)
                      for n in ("L0_ffn_w_gate", "L0_ffn_w_up", "L0_ffn_w_down")]

            block = st.enter_context(nc.Block())

            @block.sync
            def _(sp):
                sp.dma_start(x[:], a["x"][0].rearrange("(t p) d -> p t d", p=P)).then_inc(x_in, 16)
                sp.dma_start(ident[:], a["c_ident"]).then_inc(x_in, 16)
                sp.dma_start(y[:, 0], y_view[0]).then_inc(y_in[0], 16)
                sp.dma_start(wkv[:, 0], a["L0_xattn_Wk"].rearrange("(k p) n -> p k n", p=P)).then_inc(cross_in[0], 16)
                sp.dma_start(wkv[:, 1], a["L0_xattn_Wv"].rearrange("(k p) n -> p k n", p=P)).then_inc(cross_in[1], 16)
                with nc.allow_non_contiguous_dma(reason="biases, one to a partition"):
                    sp.dma_start(bq[:], a["L0_xattn_bq"].rearrange("(g p) -> p g", p=P)).then_inc(bias_in, 16)
                    sp.dma_start(bk[:], a["L0_xattn_bk"].rearrange("(g p) -> p g", p=P)).then_inc(bias_in, 16)
                sp.dma_start(y[:, 1], y_view[1]).then_inc(y_in[1], 16)
                sp.dma_start(b2[:], a["L0_xattn_b2"].partition_broadcast(P)).then_inc(b2_in, 16)

                def block_dmas(i, u, last):
                    if not last:
                        wait(sp, yT_ready, 2 * i + u + 1)
                        sp.dma_start(y[:, u], y_view[2 * i + u + 2]).then_inc(y_in[u], 16)
                    wait(sp, klo_ready, (2 * i + u + 1) * G)
                    wait(sp, khi_ready, (2 * i + u + 1) * G)
                    for s in range(HG):
                        rows = slice(s * HD, (s + 1) * HD)
                        keys = bass.ds((2 * i + u) * BLK, BLK)
                        sp.dma_start(k_hi_view[s, :, :, keys], k_hi[rows, u]).then_inc(k_out[u], 16)
                        sp.dma_start(k_lo_view[s, :, :, keys], k_lo[rows, u]).then_inc(k_out[u], 16)
                    wait(sp, vs_ready, (2 * i + u + 1) * BT)
                    sp.dma_start(v_view[:, :, bass.ds((2 * i + u) * BT * HD, BT * HD)],
                                 v[:, u].rearrange("p h t d -> p h (t d)")).then_inc(v_out[u], 16)

                def unit_load(i, w):
                    wait(sp, amax_done, 3 * i + w - 2)
                    wait(sp, qn_ready, 3 * i + w - 2)
                    sp.dma_start(w_in[:, w], w_flat[w][:, bass.ds(i * UN, UN)]).then_inc(w_unit_in[w], 16)

                def unit_store(i, w):
                    wait(sp, wq_ready, 3 * i + w + 1)
                    sp.dma_start(wq_dram[w][:, bass.ds(i * UN, UN)], w_out[:, w]).then_inc(w_unit_out[w], 16)

                for w in range(3):
                    sp.dma_start(w_in[:, w], w_flat[w][:, 0:UN]).then_inc(w_unit_in[w], 16)
                sp.dma_start(wq[:], a["L0_xattn_Wq"].rearrange("(k p) n -> p k n", p=P)).then_inc(wq_in, 16)
                def two_blocks(i):
                    block_dmas(i, 0, False)
                    block_dmas(i, 1, False)
                    for w in range(3):
                        unit_store(i, w)
                        unit_load(i + 1, w)

                two_blocks(0)
                sp.wait_ge(qhi_ready, G)
                sp.wait_ge(qlo_ready, G)
                for i in range(HG):
                    heads = q_stack[:].rearrange("p (g i) t -> p i g t", i=HG)
                    rows = slice(i * HD, (i + 1) * HD)
                    sp.dma_start(heads[0:HD, i], q_hi[rows]).then_inc(q_stacked, 16)
                    sp.dma_start(heads[HD:2 * HD, i], q_hi[rows]).then_inc(q_stacked, 16)
                    sp.dma_start(heads[2 * HD:3 * HD, i], q_lo[rows]).then_inc(q_stacked, 16)
                with sp.Fori(1, NB // 2 - 1) as i:
                    two_blocks(i)
                block_dmas(NB // 2 - 1, 0, True)
                block_dmas(NB // 2 - 1, 1, True)
                for w in range(3):
                    unit_store(NB // 2 - 1, w)
                sp.wait_ge(q_stacked, 16 * 3 * HG)
                for u in range(2):
                    sp.wait_ge(k_out[u], NB // 2 * 2 * HG * 16)
                    sp.wait_ge(v_out[u], NB // 2 * 16)
                for w in range(3):
                    sp.wait_ge(w_unit_out[w], NB // 2 * 16)

            @block.gpsimd
            def _(pool):
                nc.gpsimd.memset(ones[:], 1.0).then_inc(const_ready, 1)

                def unit(i, w):
                    wait(pool, w_unit_in[w], 16 * (i + 1))
                    wait(pool, qinv_ready, 3 * i + w + 1)
                    wait(pool, q_done, 3 * i + w)
                    blocks = w_in[:, w].rearrange("p (b e) -> p b e", e=QB)
                    nc.gpsimd.tensor_tensor(qn[:].rearrange("p (b e) -> p b e", e=QB), blocks,
                                            qinv[:].unsqueeze(2).to_broadcast([P, UB, QB]),
                                            ALU.mult).then_inc(qn_ready, 1)
                    wait(pool, q_done, 3 * i + w + 1)
                    wait(pool, w_unit_out[w], 16 * i)
                    nc.gpsimd.tensor_tensor(w_out[:, w].rearrange("p (b e) -> p b e", e=QB),
                                            q3[:].rearrange("p (b e) -> p b e", e=QB),
                                            qscale[:].unsqueeze(2).to_broadcast([P, UB, QB]),
                                            ALU.mult).then_inc(wq_ready, 1)

                pool.wait_ge(b2_in, 16)
                pool.wait_ge(xn_ready, TT)
                nc.gpsimd.tensor_tensor(x[:], x[:], b2[:].unsqueeze(1).to_broadcast([P, TT, D]), ALU.add).then_inc(x_biased, 1)
                pool.wait_ge(x_biased, 1)
                for w in range(3):
                    unit(0, w)
                with pool.Fori(1, NB // 2) as i:
                    for w in range(3):
                        unit(i, w)

            @block.scalar
            def _(act):
                layer_norm_scalar(act, var_ready, sd_ready, 1)
                act.wait_ge(yT_ready, 1)
                nc.scalar.activation(yT_hi[:, 0], yT_ps[:], ACT.Copy).then_inc(yhi_ready, 1)
                for w in range(2):
                    act.wait_ge(cross_in[w], 16)
                    nc.scalar.activation(w_hi[:, w], wkv[:, w], ACT.Copy, scale=WSCALE).then_inc(wsplit_hi, 1)
                act.wait_ge(bias_in, 32)

                def keys_out(i, u):
                    for g in range(G):
                        n = (2 * i + u) * G + g
                        wait(act, k_ready, n + 1)
                        if g == 0:
                            wait(act, k_out[u], i * 2 * HG * 16)
                        wait(act, klo_ready, n - 1 if g >= 2 else (2 * i + u) * G)
                        nc.scalar.activation(kf[:, g % 2], k_ps[:, g % 2], ACT.Identity, bias=bk[:, g:g + 1],
                                             scale=1.0 / WSCALE).then_inc(kf_ready, 1)
                        nc.scalar.activation(k_hi[:, u, g], k_ps[:, g % 2], ACT.Identity, bias=bk[:, g:g + 1],
                                             scale=1.0 / WSCALE).then_inc(khi_ready, 1)

                def y_high(i, u):
                    wait(act, yT_ready, 2 * i + u + 2)
                    wait(act, v_ready, (2 * i + u) * BT)
                    nc.scalar.activation(yT_hi[:, 1 - u], yT_ps[:], ACT.Copy).then_inc(yhi_ready, 1)

                def values_out(i, u):
                    for t in range(BT):
                        wait(act, v_ready, (2 * i + u) * BT + t + 1)
                        if t == 0:
                            wait(act, v_out[u], i * 16)
                        nc.scalar.activation(v[:, u, :, t, :], v_ps[:, t % 2].rearrange("p (h d) -> p h d", d=HD),
                                             ACT.Copy, scale=1.0 / WSCALE).then_inc(vs_ready, 1)

                def two_blocks(i, last):
                    for u in range(2):
                        keys_out(i, u)
                        if not (last and u == 1):
                            y_high(i, u)
                        values_out(i, u)

                two_blocks(0, False)
                for k in range(DK):
                    act.wait_ge(turned, k + 1)
                    nc.scalar.activation(xnT_q[:, k], v_ps[:, k % 2], ACT.Copy).then_inc(turned_out, 1)
                for g in range(G):
                    act.wait_ge(q_ready, g + 1)
                    nc.scalar.activation(qf[:, g], k_ps[:, g % 2], ACT.Identity, bias=bq[:, g:g + 1]).then_inc(qf_ready, 1)
                    nc.scalar.activation(q_hi[:, g], k_ps[:, g % 2], ACT.Identity, bias=bq[:, g:g + 1]).then_inc(qhi_ready, 1)
                with act.Fori(1, NB // 2 - 1) as i:
                    two_blocks(i, False)
                two_blocks(NB // 2 - 1, True)

            @block.vector
            def _(dve):
                chain = Chain(dve, dve_chain)
                dve.wait_ge(x_in, 32)
                nc.vector.tensor_copy(identh[:], ident[:]).then_inc(const_ready, 1)
                layer_norm_vector(dve, chain, var_ready, sd_ready, 1, xn_q, xn_ready)
                dve.wait_ge(yhi_ready, 1)
                nc.vector.tensor_tensor(yT_lo[:, 0], yT_ps[:], yT_hi[:, 0], ALU.subtract).then_inc(ylo_ready, 1)
                for w in range(2):
                    dve.wait_ge(wsplit_hi, w + 1)
                    nc.vector.scalar_tensor_tensor(out=w_lo[:, w].rearrange("p k n -> p (k n)"),
                                                   in0=wkv[:, w].rearrange("p k n -> p (k n)"), scalar=WSCALE,
                                                   in1=w_hi[:, w].rearrange("p k n -> p (k n)"),
                                                   op0=ALU.mult, op1=ALU.subtract).then_inc(wsplit_lo, 1)
                start = chain.n

                def key_low(i, u, g):
                    n = (2 * i + u) * G + g
                    wait(dve, kf_ready, n + 1)
                    wait(dve, khi_ready, n + 1)
                    nc.vector.tensor_tensor(k_lo[:, u, g], kf[:, g % 2], k_hi[:, u, g], ALU.subtract).then_inc(klo_ready, 1)

                def y_low(i, u):
                    wait(dve, yhi_ready, 2 * i + u + 2)
                    nc.vector.tensor_tensor(yT_lo[:, 1 - u], yT_ps[:], yT_hi[:, 1 - u], ALU.subtract).then_inc(ylo_ready, 1)

                def scales(i, w):
                    wait(dve, w_unit_in[w], 16 * (i + 1))
                    nc.vector.tensor_reduce(amax[:], w_in[:, w].rearrange("p (b e) -> p b e", e=QB), AX.X, ALU.max,
                                            apply_absolute_value=True).then_inc(amax_done, 1)
                    wait(dve, amax_done, 3 * i + w + 1)
                    wait(dve, wq_ready, 3 * i + w)
                    chain.link(nc.vector.tensor_scalar(qscale[:], amax[:], 1.0 / 6.0, 1e-12, ALU.mult, ALU.max))
                    chain.link(nc.vector.reciprocal(qinv[:], qscale[:]))
                    nc.vector.tensor_scalar(qinv[:], qinv[:], BELOW, None, ALU.mult).then_inc(qinv_ready, 1)

                def magnitude(i, w):
                    wait(dve, qn_ready, 3 * i + w + 1)
                    chain.link(nc.vector.tensor_scalar(qa[:].bitcast(U32), qn[:].bitcast(U32), 0x7FFFFFFF, None,
                                                       ALU.bitwise_and))
                    chain(nc.vector.tensor_scalar(q1[:], qa[:], 2.0, ROUND[0.5], ALU.min, ALU.add))

                def middle(i, w):
                    chain.link(nc.vector.tensor_scalar(q2[:], qa[:], 2.0, 4.0, ALU.max, ALU.min))
                    chain.link(nc.vector.tensor_scalar(q2[:], q2[:], ROUND[1.0], -ROUND[1.0], ALU.add, ALU.add))
                    chain.link(nc.vector.tensor_scalar(qa[:], qa[:], 4.0, ROUND[2.0], ALU.max, ALU.add))

                def grid_sum(i, w):
                    chain.link(nc.vector.scalar_tensor_tensor(out=q1[:], in0=q1[:], scalar=ROUND[0.5], in1=q2[:],
                                                              op0=ALU.subtract, op1=ALU.add))
                    chain.link(nc.vector.scalar_tensor_tensor(out=q1[:], in0=qa[:], scalar=ROUND[2.0] + 6.0, in1=q1[:],
                                                              op0=ALU.subtract, op1=ALU.add))

                def sign(i, w):
                    wait(dve, wq_ready, 3 * i + w)
                    nc.vector.scalar_tensor_tensor(out=q3[:].bitcast(U32), in0=qn[:].bitcast(U32), scalar=0x80000000,
                                                   in1=q1[:].bitcast(U32), op0=ALU.bitwise_and,
                                                   op1=ALU.bitwise_or).then_inc(q_done, 1)

                PER = 3 * 9
                PARTS = (scales, magnitude, middle, grid_sum, sign)
                STEPS = [(part, w) for w in range(3) for part in PARTS]
                AFTER_KEYS = (1, 1, 1, 0)
                AFTER_Y = (4, 5)

                def two_blocks(i, last):
                    chain.at(i * PER)
                    chain.n = start
                    steps = iter(STEPS)

                    def quantize(count):
                        for _ in range(count):
                            part, w = next(steps)
                            part(i, w)

                    for u in range(2):
                        for g in range(G):
                            key_low(i, u, g)
                            quantize(AFTER_KEYS[g])
                        if not (last and u == 1):
                            y_low(i, u)
                        quantize(AFTER_Y[u])
                    assert chain.n - start == PER and next(steps, None) is None

                two_blocks(0, False)
                for g in range(G):
                    dve.wait_ge(qf_ready, g + 1)
                    dve.wait_ge(qhi_ready, g + 1)
                    nc.vector.tensor_tensor(q_lo[:, g], qf[:, g], q_hi[:, g], ALU.subtract).then_inc(qlo_ready, 1)
                with dve.Fori(1, NB // 2 - 1) as i:
                    two_blocks(i, False)
                two_blocks(NB // 2 - 1, True)

            @block.tensor
            def _(pe):
                def turn_y(b, u):
                    pe.wait_ge(y_in[u], b)
                    for t in range(BT):
                        for c in range(CK):
                            last = nc.tensor.transpose(yT_ps[:, c, t * P:(t + 1) * P], y[:, u, t, c * P:(c + 1) * P],
                                                       ident[:])
                    last.then_inc(yT_ready, 1)

                pe.wait_ge(x_in, 32)
                turn_y(16, 0)
                pe.wait_ge(wsplit_hi, 1)
                pe.wait_ge(wsplit_lo, 1)

                def keys(i, u):
                    wait(pe, yhi_ready, 2 * i + u + 1)
                    wait(pe, ylo_ready, 2 * i + u + 1)
                    for g in range(G):
                        n = (2 * i + u) * G + g
                        wait(pe, khi_ready, n - 1 if g >= 2 else (2 * i + u) * G)
                        cols = slice(g * P, (g + 1) * P)
                        for k in range(CK):
                            nc.tensor.matmul(k_ps[:, g % 2], w_hi[:, 0, k, cols], yT_hi[:, u, k], start=k == 0, stop=False)
                            nc.tensor.matmul(k_ps[:, g % 2], w_hi[:, 0, k, cols], yT_lo[:, u, k], start=False, stop=False)
                            last = nc.tensor.matmul(k_ps[:, g % 2], w_lo[:, 0, k, cols], yT_hi[:, u, k], start=False,
                                                    stop=k == CK - 1)
                        last.then_inc(k_ready, 1)

                def values(i, u):
                    if isinstance(i, int) and i == 0 and u == 0:
                        pe.wait_ge(wsplit_hi, 2)
                        pe.wait_ge(wsplit_lo, 2)
                    for t in range(BT):
                        n = (2 * i + u) * BT + t
                        wait(pe, vs_ready, n - 1 if t >= 2 else (2 * i + u) * BT)
                        cols = slice(t * P, (t + 1) * P)
                        for k in range(CK):
                            nc.tensor.matmul(v_ps[:, t % 2], yT_hi[:, u, k, cols], w_hi[:, 1, k], start=k == 0, stop=False)
                            nc.tensor.matmul(v_ps[:, t % 2], yT_hi[:, u, k, cols], w_lo[:, 1, k], start=False, stop=False)
                            last = nc.tensor.matmul(v_ps[:, t % 2], yT_lo[:, u, k, cols], w_hi[:, 1, k], start=False,
                                                    stop=k == CK - 1)
                        last.then_inc(v_ready, 1)

                def next_y(i, u):
                    wait(pe, ylo_ready, 2 * i + u + 1)
                    turn_y(16 * (i + 1 + u), 1 - u)

                def two_blocks(i):
                    for u in range(2):
                        keys(i, u)
                        next_y(i, u)
                        values(i, u)

                two_blocks(0)
                pe.wait_ge(xn_ready, TT)
                pe.wait_ge(vs_ready, 2 * BT)
                pe.wait_ge(khi_ready, 2 * G)
                for k in range(DK):
                    if k >= 2:
                        pe.wait_ge(turned_out, k - 1)
                    for t in range(TT):
                        last = nc.tensor.transpose(v_ps[:, k % 2, t * P:(t + 1) * P], xn_q[:, t, k * P:(k + 1) * P], ident[:])
                    last.then_inc(turned, 1)
                pe.wait_ge(turned_out, DK)
                pe.wait_ge(wq_in, 16)
                for g in range(G):
                    if g >= 2:
                        pe.wait_ge(qhi_ready, g - 1)
                    for k in range(DK):
                        last = nc.tensor.matmul(k_ps[:, g % 2], wq[:, k, g * P:(g + 1) * P], xnT_q[:, k],
                                                start=k == 0, stop=k == DK - 1)
                    last.then_inc(q_ready, 1)
                pe.wait_ge(qhi_ready, G)
                with pe.Fori(1, NB // 2 - 1) as i:
                    two_blocks(i)
                i = NB // 2 - 1
                keys(i, 0)
                next_y(i, 0)
                values(i, 0)
                keys(i, 1)
                values(i, 1)

        piece = carve(late)
        w1 = piece([DK, FF])
        w2 = piece([FM, D])
        b1 = piece([FM])
        bv = piece([G])
        w1_in = sem_in(whole)("w1_in")
        w2_in = sem_in(whole)("w2_in")

        with ExitStack() as st:
            stage = "attend_"
            sb, ps, sem = sb_in(st, stage), ps_in(st, stage), sem_in(st, stage)
            k_stack = sb("k_stack", [P, 2, M], F16)
            vh = sb("vh", [P, 2, M // P, HD])
            prob = sb("prob", [P, PSLOTS, BT, T])
            sum_dve = sb("sum_dve", [P, 2, LAST_DSUM])
            sum_pool = sb("sum_pool", [P, 2, BT * T - DSUM])
            part_max = sb("part_max", [P, 2, 2, M // BLK])
            top16 = sb("top16", [P, 2, 2, 1024], F16)
            copy16 = sb("copy16", [P, 2, 1024], F16)
            top_half = sb("top_half", [P, 2, 512], F16)
            top_quarter = sb("top_quarter", [P, 2, 256], F16)
            neg_max = sb("neg_max", [P, 2, TT], F16)
            pv_sum = sb("pv_sum", [P, 2, T])
            recip = sb("recip", [P, P])
            o_out = sb("o_out", [P, 2, P])
            fold = sb("fold", [P, HD])

            s_ps = ps("s_ps", [P, 3, T])
            S_BANK = (0, 1, 2, 1)
            S_BACK = (4, 2, 4, 2)
            pre_ps = ps("pre_ps", [P, 3, BLK])
            PRE_BANK = ((0, 1), (2, 2))
            pv_ps = ps("pv_ps", [P, T])
            misc_ps = ps("misc_ps", [P, T])

            fold_in = sem("fold_in")
            ones_row = sem("ones_row")
            k_in = [[sem(f"k_in{s}{c}") for c in range(CH)] for s in range(2)]
            v_in = [sem(f"v_in{s}") for s in range(2)]
            pre_ready = [sem(f"pre_ready{b}") for b in range(2)]
            pre_read = sem("pre_read")
            pre_copied = sem("pre_copied")
            folded = sem("folded")
            fold_chain = sem("fold_chain")
            max_ready = sem("max_ready")
            row_ready = sem("row_ready")
            row_set = sem("row_set")
            s_ready = sem("s_ready")
            p_ready = sem("p_ready")
            pv_done = sem("pv_done")
            dve_summed = sem("dve_summed")
            pool_summed = sem("pool_summed")
            pv_read = sem("pv_read")
            den_ready = sem("den_ready")
            recip_ready = sem("recip_ready")
            o_ready = sem("o_ready")
            o_scaled = sem("o_scaled")
            o_stored = [sem(f"o_stored{s}") for s in range(2)]

            o_view = o_dram[:].rearrange("(h d) (t c) -> h t d c", d=HD, c=P)

            flat = prob[:].rearrange("p n t c -> p n (t c)")
            FOLDS = QUADS - 2

            PE_ORDER = ((1, 0), 0, (0, 0), 1, (0, 1), 2, (1, 1), "weighted", 3)
            ACT_ORDER = ((1, 0), 0, 1, (1, 1), 2, 3)

            def dve_columns(i, s):
                return LAST_DSUM if isinstance(i, int) and 2 * i + s == H - 1 else DSUM

            def quad_no(i, s, q):
                return 2 * QUADS * i + QUADS * s + q

            block = st.enter_context(nc.Block())
            LASTPAIR = H // 2 - 1

            @block.sync
            def _(sp):
                sp.dma_start(fold[:], a["c_fold"]).then_inc(fold_in, 16)

                def load_keys(h, s, c):
                    keys = slice(c * CHK, (c + 1) * CHK)
                    sp.dma_start(k_stack[0:2 * HD, s, keys], k_dram[h, :, keys]).then_inc(k_in[s][c], 16)
                    sp.dma_start(k_stack[2 * HD:3 * HD, s, keys], k_dram[h, 0:HD, keys]).then_inc(k_in[s][c], 16)

                def load_values(h, s):
                    sp.dma_start(vh[:, s], v_dram[h]).then_inc(v_in[s], 16)

                for s in range(2):
                    for c in range(CH):
                        load_keys(s, s, c)
                    load_values(s, s)
                sp.dma_start(w1[:], a["L0_xattn_W1"].rearrange("(k p) n -> p k n", p=P)).then_inc(w1_in, 16)
                with nc.allow_non_contiguous_dma(reason="biases, one to a partition"):
                    sp.dma_start(b1[:], a["L0_xattn_b1"].rearrange("(m p) -> p m", p=P)).then_inc(w1_in, 16)
                    sp.dma_start(bv[:], a["L0_xattn_bv"].rearrange("(g p) -> p g", p=P)).then_inc(w1_in, 16)
                sp.dma_start(w2[:], a["L0_xattn_W2"].rearrange("(k p) n -> p k n", p=P)).then_inc(w2_in, 16)

                def head(i, s, loads):
                    h = 2 * i + s
                    for c in range(CH):
                        if loads:
                            sp.wait_ge(p_ready, BT * (quad_no(i, s, QUADS // CH * (c + 1) - 1) + 1))
                            load_keys(h + 2, s, c)
                        if c == 1:
                            store_o(i, s)
                    if loads:
                        sp.wait_ge(pv_done, QUADS * (h + 1))
                        load_values(h + 2, s)

                def store_o(i, s):
                    if s == 0 and isinstance(i, int) and i == 0:
                        return
                    h = 2 * i + s - 1
                    sp.wait_ge(o_scaled, h + 1)
                    for t in range(TT):
                        sp.dma_start(o_view[h, t], o_out[t * HD:(t + 1) * HD, 1 - s]).then_inc(o_stored[1 - s], 16)

                head(0, 0, True)
                head(0, 1, True)
                with sp.Fori(1, LASTPAIR) as i:
                    head(i, 0, True)
                    head(i, 1, True)
                head(LASTPAIR, 0, False)
                head(LASTPAIR, 1, False)
                store_o(LASTPAIR + 1, 0)
                for s in range(2):
                    sp.wait_ge(o_stored[s], 16 * TT * H // 2)

            @block.tensor
            def _(pe):
                def pre(i, s, part, seen):
                    h = 2 * i + s
                    c = part // 2
                    if part % 4 == 0:
                        pe.wait_ge(k_in[s][part // 4], 32 * (i + 1))

                    def slot(b, w):
                        tt = 2 * (part % 2) + b
                        wait(pe, (pre_read, pre_copied)[b], 2 * seen + w - (b == 0))
                        keys = slice(1024 * c + BLK * w, 1024 * c + BLK * (w + 1))
                        nc.tensor.matmul(pre_ps[:, PRE_BANK[b][w]], q_stack[0:KROWS, h, tt * P:(tt + 1) * P],
                                         k_stack[0:KROWS, s, keys], start=True, stop=True).then_inc(pre_ready[b], 1)
                    return slot

                def row(i, s):
                    pe.wait_ge(max_ready, 2 * (2 * i + s + 1))
                    for t in range(TT):
                        last = nc.tensor.matmul(misc_ps[KROWS:KROWS + 1, t * P:(t + 1) * P],
                                                neg_max[:, s, t:t + 1], identh[:], start=True, stop=True)
                    last.then_inc(row_ready, 1)

                def scores(i, s, q, t):
                    h = 2 * i + s
                    if q == 0 and t == 0:
                        pe.wait_ge(row_set, h + 1)
                    n = BT * quad_no(i, s, q) + t
                    wait(pe, p_ready, n + 1 - S_BACK[t])
                    key = (BT * q + t) * P
                    last = nc.tensor.matmul(s_ps[:, S_BANK[t]], k_stack[0:KROWS + 1, s, key:key + P],
                                            q_stack[0:KROWS + 1, h, :], start=True, stop=True)
                    last.then_inc(s_ready, 1)

                def weighted(i, s, q):
                    h = 2 * i + s
                    if q == 0:
                        pe.wait_ge(v_in[s], 16 * (i + 1))
                        wait(pe, pv_read, h)
                    pe.wait_ge(p_ready, BT * (quad_no(i, s, q) + 1))
                    for t in range(BT):
                        last = nc.tensor.matmul(pv_ps[t * HD:(t + 1) * HD, :], vh[:, s, BT * q + t, :],
                                                prob[:, q % PSLOTS, t, :], start=q == 0, stop=q == QUADS - 1)
                    last.then_inc(pv_done, 1)

                def denominator(i, s):
                    h = 2 * i + s
                    pe.wait_ge(dve_summed, QUADS * (h + 1))
                    pe.wait_ge(pool_summed, QUADS * (h + 1))
                    cut = dve_columns(i, s)
                    for n in range(BT):
                        for t in range(TT):
                            col = n * T + t * P
                            part = sum_dve[:, s, col:col + P] if col < cut else sum_pool[:, s, col - cut:col - cut + P]
                            last = nc.tensor.matmul(misc_ps[t * HD:(t + 1) * HD, 0:P], ones[:], part,
                                                    start=n == 0, stop=n == BT - 1)
                    last.then_inc(den_ready, 1)

                def output(i, s):
                    h = 2 * i + s
                    pe.wait_ge(recip_ready, h + 1)
                    pe.wait_ge(pv_read, h + 1)
                    for t in range(TT):
                        last = nc.tensor.matmul(misc_ps[t * HD:(t + 1) * HD, 0:P], fold[:], pv_sum[:, s, t * P:(t + 1) * P],
                                                start=True, stop=True)
                    last.then_inc(o_ready, 1)

                def head(i, s, first, last):
                    h = 2 * i + s
                    before = (i, 0) if s else (i - 1, 1)
                    after = (i, 1) if s == 0 else (i + 1, 0)
                    for q in range(QUADS):
                        if q < QUADS - 2:
                            slot = pre(*after, q + 2, QUADS * (h + 1) + q + 2) if last >= 1 else None
                        else:
                            slot = pre(i + 1, s, q - (QUADS - 2), QUADS * (h + 1) + q + 2) if last >= 2 else None
                        for step in PE_ORDER:
                            if step == "weighted":
                                if q >= 1:
                                    weighted(i, s, q - 1)
                                elif not first:
                                    weighted(*before, QUADS - 1)
                            elif isinstance(step, int):
                                scores(i, s, q, step)
                            elif slot:
                                slot(*step)
                        if q == 2 and not first:
                            denominator(*before)
                        if q == 5 and not first:
                            output(*before)
                        if q == QUADS - 2 and last >= 1:
                            wait(pe, o_scaled, h)
                            row(*after)

                pe.wait_ge(fold_in, 16)
                for part in range(QUADS + 2):
                    slot = pre(0, part // QUADS, part % QUADS, part)
                    for t in range(4):
                        slot(t % 2, t // 2)
                    if part == QUADS - 1:
                        row(0, 0)

                pe.wait_ge(ones_row, 2)
                head(0, 0, True, 2)
                head(0, 1, False, 2)
                with pe.Fori(1, LASTPAIR) as i:
                    head(i, 0, False, 2)
                    head(i, 1, False, 2)
                head(LASTPAIR, 0, False, 1)
                head(LASTPAIR, 1, False, 0)
                weighted(LASTPAIR, 1, QUADS - 1)
                denominator(LASTPAIR, 1)
                output(LASTPAIR, 1)

            @block.scalar
            def _(act):
                def copy_row(i, s):
                    h = 2 * i + s
                    act.wait_ge(row_ready, h + 1)
                    nc.scalar.activation(q_stack[KROWS:KROWS + 1, h, :], misc_ps[KROWS:KROWS + 1, :],
                                         ACT.Copy).then_inc(row_set, 1)

                def read_pv(i, s):
                    h = 2 * i + s
                    act.wait_ge(pv_done, QUADS * (h + 1))
                    wait(act, o_ready, h - 1)
                    nc.scalar.activation(pv_sum[:, s], pv_ps[:], ACT.Copy).then_inc(pv_read, 1)

                def pre_copy(h, s, part, seen, w):
                    act.wait_ge(pre_ready[1], 2 * seen + w + 1)
                    if part < 2:
                        wait(act, max_ready, 2 * (h - 1))
                        dst = top16[:, s, part % 2]
                    else:
                        wait(act, folded, FOLDS * h + part - 3)
                        dst = copy16[:, part % 2]
                    nc.scalar.activation(dst[:, w * BLK:(w + 1) * BLK], pre_ps[:, PRE_BANK[1][w]], ACT.Copy).then_inc(pre_copied, 1)

                def head(i, s, first, last):
                    h = 2 * i + s
                    before = (i, 0) if s else (i - 1, 1)
                    after = (i, 1) if s == 0 else (i + 1, 0)
                    for q in range(QUADS):
                        Q = quad_no(i, s, q)
                        wait(act, pv_done, Q + 1 - PSLOTS)
                        wait(act, dve_summed, Q + 1 - PSLOTS)
                        wait(act, pool_summed, Q + 1 - PSLOTS)
                        for step in ACT_ORDER:
                            if isinstance(step, int):
                                act.wait_ge(s_ready, BT * Q + step + 1)
                                nc.scalar.activation(prob[:, q % PSLOTS, step, :], s_ps[:, S_BANK[step]], ACT.Exp,
                                                     scale=SCALE).then_inc(p_ready, 1)
                            elif q < QUADS - 2 and last >= 1:
                                pre_copy(h + 1, 1 - s, q + 2, QUADS * (h + 1) + q + 2, step[1])
                            elif q >= QUADS - 2 and last >= 2:
                                pre_copy(h + 2, s, q - (QUADS - 2), QUADS * (h + 1) + q + 2, step[1])
                        if q == 0 and not first:
                            read_pv(*before)
                        if q == QUADS - 2 and last >= 1:
                            copy_row(*after)

                for part in range(QUADS + 2):
                    for w in range(2):
                        pre_copy(part // QUADS, part // QUADS, part % QUADS, part, w)
                copy_row(0, 0)
                head(0, 0, True, 2)
                head(0, 1, False, 2)
                with act.Fori(1, LASTPAIR) as i:
                    head(i, 0, False, 2)
                    head(i, 1, False, 2)
                head(LASTPAIR, 0, False, 1)
                head(LASTPAIR, 1, False, 0)
                read_pv(LASTPAIR, 1)

            @block.vector
            def _(dve):
                chain = Chain(dve, fold_chain)
                HALVINGS = 2

                def pre_max(h, s, part, seen, w):
                    dve.wait_ge(pre_ready[0], 2 * seen + w + 1)
                    col = part // 2 * 2 + w
                    nc.vector.tensor_reduce(part_max[:, s, part % 2, col:col + 1], pre_ps[:, PRE_BANK[0][w]], AX.X,
                                            ALU.max).then_inc(pre_read, 1)

                def fold_in(h, s, part, seen):
                    if part >= 2:
                        dve.wait_ge(pre_copied, 2 * (seen + 1))
                        wait(dve, folded, FOLDS * h + part - 3)
                        nc.vector.tensor_tensor(top16[:, s, part % 2], top16[:, s, part % 2], copy16[:, part % 2],
                                                ALU.max).then_inc(folded, 1)

                def head_max(h, s):
                    dve.wait_ge(pre_read, 2 * QUADS * (h + 1))
                    dve.wait_ge(folded, FOLDS * (h + 1))
                    chain.n = 0
                    chain.at(HALVINGS * h)
                    wait(dve, row_ready, h - 1)
                    wait(dve, max_ready, 2 * h)
                    chain.link(nc.vector.tensor_tensor(top_half[:], top16[:, s, :, 0:512], top16[:, s, :, 512:1024], ALU.max))
                    chain.link(nc.vector.tensor_tensor(top_quarter[:], top_half[:, :, 0:256], top_half[:, :, 256:512], ALU.max))
                    tiles = neg_max[:, s].rearrange("p (a b) -> p b a", b=2)
                    nc.vector.tensor_reduce(tiles[:, 1], top_quarter[:], AX.X, ALU.max, negate=True).then_inc(max_ready, 1)
                    nc.vector.tensor_reduce(tiles[:, 0], part_max[:, s], AX.X, ALU.max, negate=True).then_inc(max_ready, 1)

                def add_up(i, s, q):
                    Q = quad_no(i, s, q)
                    cut = dve_columns(i, s)
                    if q >= 1:
                        dve.wait_ge(p_ready, BT * Q + -(-cut // T))
                    if q == 1:
                        wait(dve, den_ready, 2 * i + s - 1)
                        nc.vector.tensor_tensor(sum_dve[:, s, 0:cut], flat[:, 0, 0:cut], flat[:, 1, 0:cut],
                                                ALU.add).then_inc(dve_summed, 2)
                    elif q > 1:
                        dve.wait_ge(dve_summed, Q)
                        nc.vector.tensor_tensor(sum_dve[:, s, 0:cut], sum_dve[:, s, 0:cut], flat[:, q % PSLOTS, 0:cut],
                                                ALU.add).then_inc(dve_summed, 1)

                def invert(i, s):
                    dve.wait_ge(den_ready, 2 * i + s + 1)
                    nc.vector.reciprocal(recip[:], misc_ps[:, 0:P]).then_inc(recip_ready, 1)

                def scale_out(i, s):
                    h = 2 * i + s
                    dve.wait_ge(recip_ready, h + 1)
                    dve.wait_ge(o_ready, h + 1)
                    wait(dve, o_stored[s], 16 * TT * i)
                    nc.vector.tensor_tensor(o_out[:, s], misc_ps[:, 0:P], recip[:], ALU.mult).then_inc(o_scaled, 1)

                def head(i, s, first, last):
                    h = 2 * i + s
                    before = (i, 0) if s else (i - 1, 1)
                    for q in range(QUADS):
                        ahead = None
                        if q < QUADS - 2 and last >= 1:
                            ahead = (h + 1, 1 - s, q + 2, QUADS * (h + 1) + q + 2)
                        if q >= QUADS - 2 and last >= 2:
                            ahead = (h + 2, s, q - (QUADS - 2), QUADS * (h + 1) + q + 2)
                        if ahead:
                            pre_max(*ahead, 0)
                        add_up(i, s, q - 1)
                        if ahead:
                            pre_max(*ahead, 1)
                            fold_in(*ahead)
                        if q == QUADS - 3 and last >= 1:
                            head_max(h + 1, 1 - s)
                        if q == 2 and not first:
                            invert(*before)
                        if q == 5 and not first:
                            scale_out(*before)
                    add_up(i, s, QUADS - 1)

                for part in range(QUADS + 2):
                    for w in range(2):
                        pre_max(part // QUADS, part // QUADS, part % QUADS, part, w)
                    fold_in(part // QUADS, part // QUADS, part % QUADS, part)
                    if part == QUADS - 1:
                        head_max(0, 0)
                head(0, 0, True, 2)
                head(0, 1, False, 2)
                with dve.Fori(1, LASTPAIR) as i:
                    head(i, 0, False, 2)
                    head(i, 1, False, 2)
                head(LASTPAIR, 0, False, 1)
                head(LASTPAIR, 1, False, 0)
                invert(LASTPAIR, 1)
                scale_out(LASTPAIR, 1)

            @block.gpsimd
            def _(pool):
                for s in range(2):
                    nc.gpsimd.memset(k_stack[KROWS:KROWS + 1, s, :], 1.0).then_inc(ones_row, 1)

                def add_up(i, s, q):
                    Q = quad_no(i, s, q)
                    cut = dve_columns(i, s)
                    sums = sum_pool[:, s, 0:BT * T - cut]
                    if q:
                        pool.wait_ge(p_ready, BT * (Q + 1))
                    if q == 1:
                        wait(pool, den_ready, 2 * i + s - 1)
                        nc.gpsimd.tensor_tensor(sums, flat[:, 0, cut:], flat[:, 1, cut:],
                                                ALU.add).then_inc(pool_summed, 2)
                    elif q > 1:
                        pool.wait_ge(pool_summed, Q)
                        nc.gpsimd.tensor_tensor(sums, sums, flat[:, q % PSLOTS, cut:],
                                                ALU.add).then_inc(pool_summed, 1)

                for s in range(2):
                    for q in range(QUADS):
                        add_up(0, s, q)
                with pool.Fori(1, LASTPAIR) as i:
                    for s in range(2):
                        for q in range(QUADS):
                            add_up(i, s, q)
                for s in range(2):
                    for q in range(QUADS):
                        add_up(LASTPAIR, s, q)

        piece = carve(early)
        wqkv = piece([DK, 3 * D])
        wout = piece([DK, D])
        cos = piece([T])
        sin = piece([T])
        rot = piece([P])
        mask = piece([2 * P])
        w_in_l = sem_in(whole)("w_in_l")
        const_in = sem_in(whole)("const_in")

        with ExitStack() as st:
            stage = "mlp_"
            sb, ps, sem = sb_in(st, stage), ps_in(st, stage), sem_in(st, stage)
            oT = sb("oT", [P, DK, T])
            hT = sb("hT", [P, FM, T])
            h_ps = ps("h_ps", [P, 4, T])
            y_ps = ps("y_ps", [P, TT, D])
            o_in = sem("o_in")
            o_biased = sem("o_biased")
            h_ready = sem("h_ready")
            h_read = sem("h_read")
            y_ready = sem("y_ready")
            y_added = sem("y_added")
            block = st.enter_context(nc.Block())

            @block.sync
            def _(sp):
                sp.dma_start(oT[:], o_dram[:].rearrange("(k p) t -> p k t", p=P)).then_inc(o_in, 16)
                sp.dma_start(wqkv[:], a["L0_attn_Wqkv"].rearrange("(k p) n -> p k n", p=P)).then_inc(w_in_l, 16)
                sp.dma_start(wout[:], a["L0_attn_Wout"].rearrange("(k p) n -> p k n", p=P)).then_inc(w_in_l, 16)
                for dst, n in ((cos, "c_cos"), (sin, "c_sin"), (rot, "c_rot"), (mask, "c_mask")):
                    sp.dma_start(dst[:], a[n]).then_inc(const_in, 16)

            @block.tensor
            def _(pe):
                pe.wait_ge(o_biased, DK)
                pe.wait_ge(w1_in, 48)
                for m in range(FM):
                    wait(pe, h_read, m - 3)
                    for k in range(DK):
                        last = nc.tensor.matmul(h_ps[:, m % 4], w1[:, k, m * P:(m + 1) * P], oT[:, k],
                                                start=k == 0, stop=k == DK - 1)
                    last.then_inc(h_ready, 1)
                pe.wait_ge(w2_in, 16)
                pe.wait_ge(h_read, FM)
                for t in range(TT):
                    for k in range(FM):
                        last = nc.tensor.matmul(y_ps[:, t], hT[:, k, t * P:(t + 1) * P], w2[:, k],
                                                start=k == 0, stop=k == FM - 1)
                    last.then_inc(y_ready, 1)

            @block.scalar
            def _(act):
                act.wait_ge(w1_in, 48)
                act.wait_ge(o_in, 16)
                for k in range(DK):
                    nc.scalar.activation(oT[:, k], oT[:, k], ACT.Identity, bias=bv[:, k:k + 1]).then_inc(o_biased, 1)
                for m in range(FM):
                    act.wait_ge(h_ready, m + 1)
                    nc.scalar.activation(hT[:, m], h_ps[:, m % 4], ACT.Relu, bias=b1[:, m:m + 1]).then_inc(h_read, 1)

            @block.vector
            def _(dve):
                for t in range(TT):
                    dve.wait_ge(y_ready, t + 1)
                    nc.vector.tensor_tensor(x[:, t], x[:, t], y_ps[:, t], ALU.add).then_inc(y_added, 1)
                dve.wait_ge(y_added, TT)

        ROW_SLOTS = 8
        piece = carve(late)
        row_g = [piece([D]) for s in range(ROW_SLOTS)]
        row_in = [sem_in(whole)(f"row_in{s}") for s in range(ROW_SLOTS)]
        gate_rows = [wq_dram[w][:].rearrange("p (r c) -> (p r) c", c=D).rearrange("(m p) c -> m p c", p=P) for w in range(2)]
        down_rows = wq_dram[2][:].rearrange("p (r c) -> (p r) c", c=INNER).rearrange("(n p) c -> p n c", p=P)
        rows = [(w, m) for m in range(IK) for w in range(2)] + [(2, m) for m in range(IK)]

        def load_row(sp, n):
            w, m = rows[n]
            if w < 2:
                sp.dma_start(row_g[n % ROW_SLOTS][:], gate_rows[w][m]).then_inc(row_in[n % ROW_SLOTS], 16)
            else:
                sp.dma_start(row_g[n % ROW_SLOTS][:].rearrange("p (n c) -> p n c", c=P),
                             down_rows[:, :, m * P:(m + 1) * P]).then_inc(row_in[n % ROW_SLOTS], 16)

        with ExitStack() as st:
            stage = "local_"
            sb, ps, sem = sb_in(st, stage), ps_in(st, stage), sem_in(st, stage)
            maskb = sb("maskb", [P, 2 * P], BF16)
            identb = sb("identb", [P, P], BF16)
            xn = sb("xn", [P, TT, D])
            xnT = sb("xnT", [P, DK, T])
            qk = sb("qk", [P, 2, T])
            t_cos = sb("t_cos", [P, 2, T])
            t_sin = sb("t_sin", [P, 2, T])
            q_pad = sb("q_pad", [P, H, T])
            kT = sb("kT", [P, G, T])
            v = sb("v_local", [P, TT, D])
            KW = 3 * P
            top = sb("top", [P, 2, 2 * D // P])
            bias = sb("bias", [P, 2, 2 * D // P])
            total = sb("total", [P, 2, H])
            inv = sb("inv", [P, 2, H])
            pr = sb("pr", [P, 3, 2, D])
            prT = sb("prT", [P, 4, 2, D])
            oT = sb("oT_local", [P, G, T])
            s_ps = ps("sl_ps", [P, 2, 2, D])
            t_ps = ps("t_ps", [P, 2, D])
            o_ps = ps("ol_ps", [P, 2, D])

            consts = sem("consts")
            padded = sem("padded")
            turned = sem("turned_l")
            turned_out = sem("turned_out_l")
            qk_ready = sem("qk_ready")
            qk_out = sem("qk_out")
            rot_ready = sem("rot_ready")
            cos_done = sem("cos_done")
            roped = sem("roped")
            v_ready = sem("v_ready_l")
            v_read = sem("v_read_l")
            s_ready = sem("s_ready_l")
            top_ready = sem("top_ready")
            bias_ready = sem("bias_ready")
            p_ready = sem("p_ready_l")
            inv_ready = sem("inv_ready")
            p_scaled = sem("p_scaled")
            pT_ready = sem("pT_ready")
            pT_read = sem("pT_read")
            o_ready = sem("o_ready_l")
            o_read = sem("o_read_l")
            y_ready = sem("y_ready_l")
            y_added = sem("y_added_l")
            dve_chain = sem("dve_chain_l")
            seen = [(max(0, t - WINDOW // P), min(t, WINDOW // P) + 1) for t in range(TT)]
            per_bank = [D // (nk * P) for _, nk in seen]
            units = [(t, h) for t in range(TT) for h in range(0, H, 2 * per_bank[t])]
            heads = [2 * per_bank[t] for t, _ in units]
            upto = [sum(heads[:n + 1]) for n in range(len(units))]
            groups_of = [[g for g in range(G) if h < (g + 1) * HG <= h + heads[n]] for n, (t, h) in enumerate(units)]
            closes = {n: t for n, (t, h) in enumerate(units) if h + heads[n] == H}

            def place(n, j):
                t, h = units[n]
                return j // per_bank[t], j % per_bank[t] * seen[t][1] * P

            def used(n):
                t = units[n][0]
                return per_bank[t] * seen[t][1] * P
            block = st.enter_context(nc.Block())

            @block.sync
            def _(sp):
                for n in range(ROW_SLOTS):
                    load_row(sp, n)

            @block.gpsimd
            def _(pool):
                nc.gpsimd.memset(q_pad[:], 0.0).then_inc(padded, 1)
                pool.wait_ge(const_in, 64)
                nc.gpsimd.tensor_copy(maskb[:], mask[:]).then_inc(consts, 1)
                nc.gpsimd.tensor_copy(identb[:], ident[:]).then_inc(consts, 1)
                for m in range(2 * G):
                    pool.wait_ge(qk_out, m + 1)
                    wait(pool, roped, m - 1)
                    nc.gpsimd.tensor_tensor(t_cos[:, m % 2], qk[:, m % 2], cos[:], ALU.mult).then_inc(cos_done, 1)

            @block.scalar
            def _(act):
                layer_norm_scalar(act, var_ready, sd_ready, 2)
                for m in range(2 * G):
                    act.wait_ge(qk_ready, m + 1)
                    wait(act, roped, m - 1)
                    nc.scalar.activation(qk[:, m % 2], s_ps[:, 0, m % 2], ACT.Copy).then_inc(qk_out, 1)
                for t in range(TT):
                    act.wait_ge(v_ready, t + 1)
                    nc.scalar.activation(v[:, t], t_ps[:, t % 2], ACT.Copy).then_inc(v_read, 1)

                def turn_out(n):
                    t, h = units[n]
                    act.wait_ge(pT_ready, n + 1)
                    if n >= 4:
                        act.wait_ge(o_ready, sum(len(g) for g in groups_of[:n - 3]))
                    nc.scalar.activation(prT[:, n % 4, :, 0:used(n)], t_ps[:, :, 0:used(n)], ACT.Copy).then_inc(pT_read, 1)

                def exps(n):
                    t, h = units[n]
                    act.wait_ge(bias_ready, n + 1)
                    wait(act, pT_ready, n - 2)
                    if h == 0 and t >= 2:
                        act.wait_ge(inv_ready, n - 1)
                    for j in range(heads[n]):
                        b, col = place(n, j)
                        w = seen[t][1] * P
                        nc.scalar.activation(pr[:, n % 3, b, col:col + w], s_ps[:, n % 2, b, col:col + w], ACT.Exp,
                                             bias=bias[:, n % 2, j:j + 1], scale=SCALE,
                                             accum_out=total[:, t % 2, h + j:h + j + 1]).then_inc(p_ready, 1)

                for n in range(len(units) + 2):
                    if n >= 2:
                        turn_out(n - 2)
                    if n < len(units):
                        exps(n)

            @block.vector
            def _(dve):
                chain = Chain(dve, dve_chain)
                layer_norm_vector(dve, chain, var_ready, sd_ready, 2, xn, xn_ready)
                for k in range(DK):
                    dve.wait_ge(turned, k + 1)
                    nc.vector.tensor_copy(xnT[:, k], s_ps[:, 1, k % 2]).then_inc(turned_out, 1)
                dve.wait_ge(const_in, 64)
                dve.wait_ge(padded, 1)
                for m in range(2 * G):
                    dve.wait_ge(rot_ready, m + 1)
                    wait(dve, roped, m - 1)
                    chain.link(nc.vector.tensor_tensor(t_sin[:, m % 2], s_ps[:, 1, m % 2], sin[:], ALU.mult))
                    dve.wait_ge(cos_done, m + 1)
                    if m < G:
                        for i in range(HG):
                            rows = slice(i * HD, (i + 1) * HD)
                            last = nc.vector.tensor_tensor(q_pad[rows, m * HG + i], t_cos[rows, m % 2], t_sin[rows, m % 2],
                                                           ALU.add)
                            if i < HG - 1:
                                chain(last)
                        last.then_inc(roped, 1)
                    else:
                        nc.vector.tensor_tensor(kT[:, m - G], t_cos[:, m % 2], t_sin[:, m % 2], ALU.add).then_inc(roped, 1)

                def maxima(n):
                    t, h = units[n]
                    dve.wait_ge(s_ready, n + 1)
                    wait(dve, bias_ready, n - 1)
                    nc.vector.tensor_reduce(top[:, n % 2, 0:heads[n]].rearrange("p (b j) -> p b j", b=2),
                                            s_ps[:, n % 2, :, 0:used(n)].rearrange("p b (j w) -> p b j w", j=per_bank[t]),
                                            AX.X, ALU.max, negate=True).then_inc(top_ready, 1)
                    dve.wait_ge(top_ready, n + 1)
                    if n >= 2:
                        dve.wait_ge(p_ready, upto[n - 2])
                    nc.vector.tensor_scalar(bias[:, n % 2, 0:heads[n]], top[:, n % 2, 0:heads[n]], SCALE, None,
                                            ALU.mult).then_inc(bias_ready, 1)

                def normalise(n):
                    t, h = units[n]
                    dve.wait_ge(p_ready, upto[n])
                    if n >= 1:
                        dve.wait_ge(p_scaled, upto[n - 1])
                    nc.vector.reciprocal(inv[:, t % 2, h:h + heads[n]], total[:, t % 2, h:h + heads[n]]).then_inc(inv_ready, 1)
                    dve.wait_ge(inv_ready, n + 1)
                    for j in range(heads[n]):
                        b, col = place(n, j)
                        w = seen[t][1] * P
                        nc.vector.tensor_scalar(pr[:, n % 3, b, col:col + w], pr[:, n % 3, b, col:col + w],
                                                inv[:, t % 2, h + j:h + j + 1], None, ALU.mult).then_inc(p_scaled, 1)

                def out_copy(t):
                    dve.wait_ge(o_ready, G * (t + 1))
                    nc.vector.tensor_copy(oT[:, :, t * P:(t + 1) * P],
                                          o_ps[:, t % 2].rearrange("p (g q) -> p g q", g=G)).then_inc(o_read, 1)

                def add(t):
                    dve.wait_ge(y_ready, t + 1)
                    nc.vector.tensor_tensor(x[:, t], x[:, t], o_ps[:, t % 2], ALU.add).then_inc(y_added, 1)

                for n in range(len(units) + 6):
                    if n < len(units):
                        maxima(n)
                    if 1 <= n <= len(units):
                        normalise(n - 1)
                    if n - 4 in closes:
                        out_copy(closes[n - 4])
                    if n - 6 in closes:
                        add(closes[n - 6])
                dve.wait_ge(y_added, TT)

            @block.tensor
            def _(pe):
                pe.wait_ge(xn_ready, 2 * TT)
                for k in range(DK):
                    wait(pe, turned_out, k - 1)
                    for t in range(TT):
                        last = nc.tensor.transpose(s_ps[:, 1, k % 2, t * P:(t + 1) * P], xn[:, t, k * P:(k + 1) * P],
                                                   ident[:])
                    last.then_inc(turned, 1)
                pe.wait_ge(turned_out, DK)
                pe.wait_ge(w_in_l, 32)
                pe.wait_ge(const_in, 64)

                def rotate(m):
                    pe.wait_ge(qk_out, m + 1)
                    wait(pe, roped, m - 1)
                    nc.tensor.matmul(s_ps[:, 1, m % 2], rot[:], qk[:, m % 2], start=True, stop=True).then_inc(rot_ready, 1)

                for m in range(2 * G):
                    wait(pe, qk_out, m - 1)
                    for k in range(DK):
                        last = nc.tensor.matmul(s_ps[:, 0, m % 2], wqkv[:, k, m * P:(m + 1) * P], xnT[:, k],
                                                start=k == 0, stop=k == DK - 1)
                    last.then_inc(qk_ready, 1)
                    if m >= 1:
                        rotate(m - 1)
                rotate(2 * G - 1)
                for t in range(TT):
                    wait(pe, v_read, t - 1)
                    for k in range(DK):
                        last = nc.tensor.matmul(t_ps[:, t % 2], xnT[:, k, t * P:(t + 1) * P], wqkv[:, k, 2 * D:3 * D],
                                                start=k == 0, stop=k == DK - 1)
                    last.then_inc(v_ready, 1)
                pe.wait_ge(v_read, TT)
                pe.wait_ge(roped, 2 * G)
                pe.wait_ge(consts, 2)

                def local_scores(n):
                    t, h = units[n]
                    k0, nk = seen[t]
                    if n >= 2:
                        pe.wait_ge(p_ready, upto[n - 2])
                    for j in range(heads[n]):
                        b, col = place(n, j)
                        nc.tensor.matmul(s_ps[:, n % 2, b, col:col + nk * P], q_pad[:, h + j, t * P:(t + 1) * P],
                                         kT[:, (h + j) // HG, k0 * P:(k0 + nk) * P], start=True, stop=False)
                        if t >= WINDOW // P:
                            nc.tensor.matmul(s_ps[:, n % 2, b, col:col + P], identb[:], maskb[:, P:2 * P], start=False,
                                             stop=False)
                        last = nc.tensor.matmul(s_ps[:, n % 2, b, col + (nk - 1) * P:col + nk * P], identb[:], maskb[:, 0:P],
                                                start=False, stop=True)
                    last.then_inc(s_ready, 1)

                def turn(n):
                    t, h = units[n]
                    pe.wait_ge(p_scaled, upto[n])
                    wait(pe, pT_read, n)
                    for b in range(2):
                        for col in range(0, used(n), P):
                            last = nc.tensor.transpose(t_ps[:, b, col:col + P], pr[:, n % 3, b, col:col + P], ident[:])
                    last.then_inc(pT_ready, 1)

                def values(n):
                    t, h = units[n]
                    k0, nk = seen[t]
                    pe.wait_ge(pT_read, n + 1)
                    wait(pe, y_added, t - 1)
                    for g in groups_of[n]:
                        for k in range(nk):
                            for i in range(HG):
                                head = g * HG + i
                                m = n - (h - head + heads[n] - 1) // heads[n]
                                b, col = place(m, head - units[m][1])
                                last = nc.tensor.matmul(o_ps[i * HD:(i + 1) * HD, t % 2, g * P:(g + 1) * P],
                                                        v[:, k0 + k, head * HD:(head + 1) * HD],
                                                        prT[:, m % 4, b, col + k * P:col + (k + 1) * P],
                                                        start=k == 0, stop=k == nk - 1)
                        last.then_inc(o_ready, 1)

                def back(t):
                    pe.wait_ge(o_read, t + 1)
                    for k in range(DK):
                        last = nc.tensor.matmul(o_ps[:, t % 2], oT[:, k, t * P:(t + 1) * P], wout[:, k],
                                                start=k == 0, stop=k == DK - 1)
                    last.then_inc(y_ready, 1)

                for n in range(len(units) + 6):
                    if n < len(units):
                        local_scores(n)
                    if 0 <= n - 2 < len(units):
                        turn(n - 2)
                    if 0 <= n - 3 < len(units):
                        values(n - 3)
                    if n - 5 in closes:
                        back(closes[n - 5])

        with ExitStack() as st:
            stage = "ffn_"
            sb, ps, sem = sb_in(st, stage), ps_in(st, stage), sem_in(st, stage)
            wT = [sb("wgT", [P, DK, INNER]), sb("wuT", [P, DK, INNER])]
            wdT = sb("wdT", [P, IK, D])
            xn = sb("xn_f", [P, D * TT])
            xq = sb("xq", [P, D * TT])
            xqT = sb("xqT", [P, DK, T])
            hT = sb("hqT", [P, IK, P])
            h = sb("h", [P, 512])
            hq = sb("hq", [P, 2, INNER])
            gate = sb("gate", [P, 2, 512])
            NQ = 512
            amax = sb("amax_f", [P, NQ // QB])
            qscale = sb("qscale_f", [P, NQ // QB])
            qinv = sb("qinv_f", [P, NQ // QB])
            qn = sb("qn_f", [P, NQ])
            qa = sb("qa_f", [P, NQ])
            q1 = sb("q1_f", [P, NQ])
            q2 = sb("q2_f", [P, NQ])
            w_ps = ps("w_ps", [P, 2, D])
            g_ps = ps("g_ps", [P, 2, D])
            u_ps = ps("u_ps", [P, 2, D])
            y_ps = ps("yf_ps", [P, 2, D])

            w_turned = sem("w_turned")
            w_out = sem("w_out_f")
            xq_ready = sem("xq_ready")
            gate_ready = sem("gate_ready")
            silu_ready = sem("silu_ready")
            gu_read = sem("gu_read")
            hq_ready = sem("hq_ready")
            y_ready = sem("y_ready_f")
            y_added = sem("y_added_f")
            stored = sem("stored")
            dve_chain = sem("dve_chain_f")

            cuts = [(0, 512), (512, 1024), (1024, INNER)]
            FIRST = 8
            turns = [("w", n) for n in range(FIRST)] + [("x", 0)] + [("w", n) for n in range(FIRST, len(rows))]
            for t in range(1, TT):
                turns += [("x", t)] + [("h", t - 1, c) for c in range(3)]
            turns += [("h", TT - 1, c) for c in range(3)]
            number = {turn: n for n, turn in enumerate(turns)}
            last_row = [2 * (hi // P) - 1 for _, hi in cuts]
            block = st.enter_context(nc.Block())

            @block.sync
            def _(sp):
                for n in range(ROW_SLOTS, len(rows)):
                    sp.wait_ge(w_turned, number[("w", n - ROW_SLOTS)] + 1)
                    load_row(sp, n)
                for t in range(TT):
                    sp.wait_ge(y_added, t + 1)
                    sp.dma_start(out[0, t * P:(t + 1) * P, :], x[:, t]).then_inc(stored, 16)
                sp.wait_ge(stored, 16 * TT)

            @block.scalar
            def _(act):
                layer_norm_scalar(act, var_ready, sd_ready, 3)

                def copy_out(*turn):
                    n = number[turn]
                    act.wait_ge(w_turned, n + 1)
                    src = w_ps[:, n % 2]
                    if turn[0] == "w":
                        w, m = rows[turn[1]]
                        if w < 2:
                            dst, src = wT[w][:, :, m * P:(m + 1) * P], src.rearrange("p (k c) -> p k c", c=P)
                        else:
                            dst = wdT[:, m]
                    elif turn[0] == "x":
                        dst, src = xqT[:, :, turn[1] * P:(turn[1] + 1) * P], src.rearrange("p (k c) -> p k c", c=P)
                    else:
                        t, (lo, hi) = turn[1], cuts[turn[2]]
                        wait(act, y_ready, t)
                        dst, src = hT[:, lo // P:hi // P].rearrange("p k c -> p (k c)"), src[:, 0:hi - lo]
                    nc.scalar.activation(dst, src, ACT.Copy).then_inc(w_out, 1)

                def silu(t, c):
                    n, w = 3 * t + c, cuts[c][1] - cuts[c][0]
                    act.wait_ge(gate_ready, n + 1)
                    wait(act, gu_read, n - 1)
                    nc.scalar.activation(gate[:, n % 2, 0:w], g_ps[:, n % 2, 0:w], ACT.Silu).then_inc(silu_ready, 1)

                for n in range(FIRST):
                    copy_out("w", n)
                copy_out("x", 0)
                for c in range(3):
                    for n in range(FIRST * (c + 1), FIRST * (c + 2)):
                        copy_out("w", n)
                    silu(0, c)
                for n in range(4 * FIRST, len(rows)):
                    copy_out("w", n)
                for t in range(1, TT):
                    copy_out("x", t)
                    for c in range(3):
                        silu(t, c)
                    for c in range(3):
                        copy_out("h", t - 1, c)
                for c in range(3):
                    copy_out("h", TT - 1, c)

            @block.vector
            def _(dve):
                chain = Chain(dve, dve_chain)

                def quantize(src, dst, n, ready):
                    def blocks(ap):
                        return ap.rearrange("p (b e) -> p b e", e=QB)
                    nb = n // QB
                    def each(s):
                        return s[:, 0:nb].unsqueeze(2).to_broadcast([P, nb, QB])
                    chain.link(nc.vector.tensor_reduce(amax[:, 0:nb], blocks(src), AX.X, ALU.max, apply_absolute_value=True))
                    chain.link(nc.vector.tensor_scalar(qscale[:, 0:nb], amax[:, 0:nb], 1.0 / 6.0, 1e-12, ALU.mult, ALU.max))
                    chain.link(nc.vector.reciprocal(qinv[:, 0:nb], qscale[:, 0:nb]))
                    chain.link(nc.vector.tensor_scalar(qinv[:, 0:nb], qinv[:, 0:nb], BELOW, None, ALU.mult))
                    chain.link(nc.vector.tensor_tensor(blocks(qn[:, 0:n]), blocks(src), each(qinv), ALU.mult))
                    chain.link(nc.vector.tensor_scalar(qa[:, 0:n].bitcast(U32), qn[:, 0:n].bitcast(U32), 0x7FFFFFFF, None,
                                                       ALU.bitwise_and))
                    chain(nc.vector.tensor_scalar(q1[:, 0:n], qa[:, 0:n], 2.0, ROUND[0.5], ALU.min, ALU.add))
                    chain.link(nc.vector.tensor_scalar(q2[:, 0:n], qa[:, 0:n], 2.0, 4.0, ALU.max, ALU.min))
                    chain.link(nc.vector.tensor_scalar(q2[:, 0:n], q2[:, 0:n], ROUND[1.0], -ROUND[1.0], ALU.add, ALU.add))
                    chain(nc.vector.tensor_scalar(qa[:, 0:n], qa[:, 0:n], 4.0, ROUND[2.0], ALU.max, ALU.add))
                    chain.link(nc.vector.scalar_tensor_tensor(out=q1[:, 0:n], in0=q1[:, 0:n], scalar=ROUND[0.5],
                                                              in1=q2[:, 0:n], op0=ALU.subtract, op1=ALU.add))
                    chain.link(nc.vector.scalar_tensor_tensor(out=q1[:, 0:n], in0=qa[:, 0:n], scalar=ROUND[2.0] + 6.0,
                                                              in1=q1[:, 0:n], op0=ALU.subtract, op1=ALU.add))
                    chain.link(nc.vector.scalar_tensor_tensor(out=q1[:, 0:n].bitcast(U32), in0=qn[:, 0:n].bitcast(U32),
                                                              scalar=0x80000000, in1=q1[:, 0:n].bitcast(U32),
                                                              op0=ALU.bitwise_and, op1=ALU.bitwise_or))
                    nc.vector.tensor_tensor(blocks(dst), blocks(q1[:, 0:n]), each(qscale), ALU.mult).then_inc(ready, 1)

                xn_t = xn[:].rearrange("p (t d) -> p t d", t=TT)
                layer_norm_vector(dve, chain, var_ready, sd_ready, 3, xn_t, xn_ready)

                def quantize_x(t):
                    dve.wait_ge(xn_ready, 2 * TT + t + 1)
                    cols = slice(t * D, (t + 1) * D)
                    quantize(xn[:, cols], xq[:, cols], D, xq_ready)
                    dve.wait_ge(xq_ready, t + 1)

                def quantize_h(t, c):
                    n, (lo, hi) = 3 * t + c, cuts[c]
                    dve.wait_ge(silu_ready, n + 1)
                    nc.vector.tensor_tensor(h[:, 0:hi - lo], gate[:, n % 2, 0:hi - lo], u_ps[:, n % 2, 0:hi - lo],
                                            ALU.mult).then_inc(gu_read, 1)
                    dve.wait_ge(gu_read, n + 1)
                    if t >= 2:
                        dve.wait_ge(w_turned, number[("h", t - 2, c)] + 1)
                    quantize(h[:, 0:hi - lo], hq[:, t % 2, lo:hi], hi - lo, hq_ready)
                    dve.wait_ge(hq_ready, n + 1)

                def add_out(t):
                    dve.wait_ge(y_ready, t + 1)
                    nc.vector.tensor_tensor(x[:, t], x[:, t], y_ps[:, t % 2], ALU.add).then_inc(y_added, 1)

                quantize_x(0)
                quantize_x(1)
                for t in range(TT):
                    for c in range(3):
                        quantize_h(t, c)
                    if t + 2 < TT:
                        quantize_x(t + 2)
                    if t >= 1:
                        add_out(t - 1)
                add_out(TT - 1)

            @block.tensor
            def _(pe):
                def turn(*what):
                    n = number[what]
                    wait(pe, w_out, n - 1)
                    if what[0] == "w":
                        s = what[1] % ROW_SLOTS
                        pe.wait_ge(row_in[s], 16 * (what[1] // ROW_SLOTS + 1))
                        tiles = [row_g[s][:, k * P:(k + 1) * P] for k in range(DK)]
                    elif what[0] == "x":
                        pe.wait_ge(xq_ready, what[1] + 1)
                        tiles = [xq[:, what[1] * D + k * P:what[1] * D + (k + 1) * P] for k in range(DK)]
                    else:
                        t, (lo, hi) = what[1], cuts[what[2]]
                        pe.wait_ge(hq_ready, 3 * t + what[2] + 1)
                        tiles = [hq[:, t % 2, col:col + P] for col in range(lo, hi, P)]
                    for k, tile in enumerate(tiles):
                        last = nc.tensor.transpose(w_ps[:, n % 2, k * P:(k + 1) * P], tile, ident[:])
                    last.then_inc(w_turned, 1)

                def gate_up(t):
                    for c, (lo, hi) in enumerate(cuts):
                        n = 3 * t + c
                        pe.wait_ge(w_out, max(number[("w", last_row[c])], number[("x", t)]) + 1)
                        wait(pe, gu_read, n - 1)
                        for b, bank in enumerate((g_ps, u_ps)):
                            for k in range(DK):
                                if t == 0:
                                    turn("w", FIRST * (c + 1) + DK * b + k)
                                last = nc.tensor.matmul(bank[:, n % 2, 0:hi - lo], xqT[:, k, t * P:(t + 1) * P],
                                                        wT[b][:, k, lo:hi], start=k == 0, stop=k == DK - 1)
                        last.then_inc(gate_ready, 1)

                def down(t):
                    for c in range(3):
                        turn("h", t, c)
                    wait(pe, y_added, t - 1)
                    for c, (lo, hi) in enumerate(cuts):
                        pe.wait_ge(w_out, number[("h", t, c)] + 1)
                        for k in range(lo // P, hi // P):
                            last = nc.tensor.matmul(y_ps[:, t % 2], hT[:, k], wdT[:, k], start=k == 0, stop=k == IK - 1)
                    last.then_inc(y_ready, 1)

                for n in range(FIRST):
                    turn("w", n)
                turn("x", 0)
                gate_up(0)
                for n in range(4 * FIRST, len(rows)):
                    turn("w", n)
                for t in range(1, TT):
                    turn("x", t)
                    gate_up(t)
                    down(t - 1)
                down(TT - 1)


_INS = ["x", "ctx_768", "L0_xattn_Wq", "L0_xattn_bq", "L0_xattn_Wk", "L0_xattn_bk", "L0_xattn_Wv", "L0_xattn_bv",
        "L0_xattn_W1", "L0_xattn_b1", "L0_xattn_W2", "L0_xattn_b2", "L0_attn_Wqkv", "L0_attn_Wout",
        "L0_ffn_w_gate", "L0_ffn_w_up", "L0_ffn_w_down"]


def kernel(**inputs):
    import numpy as _np
    import concourse.bacc as _bacc
    from concourse import mybir as _mybir
    from concourse.bass_utils import run_bass_kernel_spmd as _run

    nc = _bacc.Bacc("TRN2", target_bir_lowering=False, num_devices=1)
    named = {n: _np.ascontiguousarray(inputs[n]) for n in _INS}
    named.update({"c_" + n: c for n, c in constants().items()})
    arrays, args = {}, {}
    for name, array in named.items():
        arrays[f"in_{name}_dram"] = array
        args[name] = nc.dram_tensor(f"in_{name}_dram", array.shape, _mybir.dt.from_np(array.dtype),
                                    kind="ExternalInput").ap()
    out = nc.dram_tensor("out_0_dram", (1, T, D), _mybir.dt.float32, kind="ExternalOutput").ap()
    perceiver(nc, args, out)
    r = _run(nc, [arrays], core_ids=[0])
    return r.results[0]["out_0_dram"]
```
